# Optimizing a Trainium2 kernel written in Bass

```python
import numpy as np
import jax
import jax.numpy as jnp

def _softmax(x, axis=-1):
    return jax.nn.softmax(x, axis=axis)

def _gelu(x):
    return jax.nn.gelu(x, approximate=True)

def _silu(x):
    return jax.nn.silu(x)

def _sigmoid(x):
    return jax.nn.sigmoid(x)

def _layernorm(x, axis=-1, eps=1e-05):
    m = jnp.mean(x, axis=axis, keepdims=True)
    v = jnp.var(x, axis=axis, keepdims=True)
    return (x - m) / jnp.sqrt(v + eps)

def _scatter_add(tgt, idx, src, axis=0):
    return tgt.at[idx].add(src)

def _segment_sum(src, seg, n):
    return jax.ops.segment_sum(src, seg, n)
kernel_name = 'mk_recurrent_d2_jaxref_r4_5d888d'

def setup_inputs(seed: int=0):
    np.random.seed(seed)
    _w = jnp.asarray

    def _L0_attn_setup():
        import jax, jax.numpy as jnp
        import numpy as np
        DT_MIN, DT_MAX, STAB_EPS, RMS_EPS = (0.0001, 10.0, 1e-08, 1e-06)

        def soft_clamp(x, mn=DT_MIN, mx=DT_MAX):
            center = (mx + mn) / 2.0
            half = (mx - mn) / 2.0
            return center + half * jnp.tanh((x - center) / half)
        key = jax.random.key(seed)
        ks = jax.random.split(key, 8)
        B, L, D, N = (1, 1024, 256, 16)
        s = D ** (-0.5)
        x = jax.random.normal(ks[0], (B, L, D), jnp.float32)
        A_log = jnp.broadcast_to(jnp.log(jnp.arange(1, N + 1, dtype=jnp.float32)), (D, N))
        W_delta = jax.random.normal(ks[1], (D, D), jnp.float32) * s
        b_delta = jax.random.normal(ks[2], (D,), jnp.float32) * 0.1
        W_B = jax.random.normal(ks[3], (D, N), jnp.float32) * s
        W_C = jax.random.normal(ks[4], (D, N), jnp.float32) * s
        D_skip = jax.random.normal(ks[5], (D,), jnp.float32) * 0.1 + 1.0
        norm_weight = jnp.ones((D,), jnp.float32)
        return {'x': x, 'A_log': A_log, 'W_delta': W_delta, 'b_delta': b_delta, 'W_B': W_B, 'W_C': W_C, 'D_skip': D_skip, 'norm_weight': norm_weight}
    _L0_attn_in = _L0_attn_setup()

    def _L0_ffn_setup():
        import jax, jax.numpy as jnp
        import numpy as np
        D_MODEL = 256
        EXPERT_DIM = 128
        N_EXPERTS = 8
        TOP_K = 2

        def _sq_relu(h):
            return jnp.square(jax.nn.relu(h))
        key = jax.random.key(seed)
        ks = jax.random.split(key, 6)
        s = 0.02
        x = jax.random.normal(ks[0], (2, 512, D_MODEL), dtype=jnp.float32)
        Ws1 = jax.random.normal(ks[1], (D_MODEL, EXPERT_DIM), dtype=jnp.float32) * s
        Ws2 = jax.random.normal(ks[2], (EXPERT_DIM, D_MODEL), dtype=jnp.float32) * s
        W1 = jax.random.normal(ks[3], (N_EXPERTS, D_MODEL, EXPERT_DIM), dtype=jnp.float32) * s
        W2 = jax.random.normal(ks[4], (N_EXPERTS, EXPERT_DIM, D_MODEL), dtype=jnp.float32) * s
        Wr = jax.random.normal(ks[5], (D_MODEL, N_EXPERTS), dtype=jnp.float32) * s
        return {'x': x, 'Ws1': Ws1, 'Ws2': Ws2, 'W1': W1, 'W2': W2, 'Wr': Wr}
    _L0_ffn_in = _L0_ffn_setup()

    def _L1_attn_setup():
        import jax, jax.numpy as jnp
        import numpy as np
        EMBED_DIM = 256
        NUM_HEADS = 16
        EFF_HEADS = NUM_HEADS // 2
        HEAD_DIM = EMBED_DIM // NUM_HEADS
        LAMBDA_INIT = 0.8
        B, N = (2, 512)
        key = jax.random.key(seed)
        ks = jax.random.split(key, 14)
        s = 0.02
        return {'x': jax.random.normal(ks[0], (B, N, EMBED_DIM), dtype=jnp.float32), 'Wq': jax.random.normal(ks[1], (EMBED_DIM, EMBED_DIM), dtype=jnp.float32) * s, 'bq': jnp.zeros((EMBED_DIM,), dtype=jnp.float32), 'Wk': jax.random.normal(ks[2], (EMBED_DIM, EMBED_DIM), dtype=jnp.float32) * s, 'bk': jnp.zeros((EMBED_DIM,), dtype=jnp.float32), 'Wv': jax.random.normal(ks[3], (EMBED_DIM, EMBED_DIM), dtype=jnp.float32) * s, 'bv': jnp.zeros((EMBED_DIM,), dtype=jnp.float32), 'Wp': jax.random.normal(ks[4], (EMBED_DIM, EMBED_DIM), dtype=jnp.float32) * s, 'bp': jnp.zeros((EMBED_DIM,), dtype=jnp.float32), 'lambda_q1': jax.random.normal(ks[5], (EFF_HEADS, 1, HEAD_DIM), dtype=jnp.float32) * s, 'lambda_k1': jax.random.normal(ks[6], (EFF_HEADS, 1, HEAD_DIM), dtype=jnp.float32) * s, 'lambda_q2': jax.random.normal(ks[7], (EFF_HEADS, 1, HEAD_DIM), dtype=jnp.float32) * s, 'lambda_k2': jax.random.normal(ks[8], (EFF_HEADS, 1, HEAD_DIM), dtype=jnp.float32) * s}
    _L1_attn_in = _L1_attn_setup()

    def _L1_ffn_setup():
        import jax, jax.numpy as jnp
        import numpy as np
        B, C, D = (2, 512, 256)
        I = 512
        E, K = (8, 2)
        CF = 1.25
        key = jax.random.key(seed)
        k1, k2, k3, k4 = jax.random.split(key, 4)
        scale = 0.02
        return {'hidden_states': jax.random.normal(k1, (B, C, D), jnp.float32), 'Wg': jax.random.normal(k2, (E, D), jnp.float32) * scale, 'W1': jax.random.normal(k3, (E, D, 2 * I), jnp.float32) * scale, 'W2': jax.random.normal(k4, (E, I, D), jnp.float32) * scale}
    _L1_ffn_in = _L1_ffn_setup()
    _d = {'L0_attn_x': _L0_attn_in['x'], 'L0_attn_A_log': _L0_attn_in['A_log'], 'L0_attn_W_delta': _L0_attn_in['W_delta'], 'L0_attn_b_delta': _L0_attn_in['b_delta'], 'L0_attn_W_B': _L0_attn_in['W_B'], 'L0_attn_W_C': _L0_attn_in['W_C'], 'L0_attn_D_skip': _L0_attn_in['D_skip'], 'L0_attn_norm_weight': _L0_attn_in['norm_weight'], 'L0_ffn_Ws1': _L0_ffn_in['Ws1'], 'L0_ffn_Ws2': _L0_ffn_in['Ws2'], 'L0_ffn_W1': _L0_ffn_in['W1'], 'L0_ffn_W2': _L0_ffn_in['W2'], 'L0_ffn_Wr': _L0_ffn_in['Wr'], 'L1_attn_Wq': _L1_attn_in['Wq'], 'L1_attn_bq': _L1_attn_in['bq'], 'L1_attn_Wk': _L1_attn_in['Wk'], 'L1_attn_bk': _L1_attn_in['bk'], 'L1_attn_Wv': _L1_attn_in['Wv'], 'L1_attn_bv': _L1_attn_in['bv'], 'L1_attn_Wp': _L1_attn_in['Wp'], 'L1_attn_bp': _L1_attn_in['bp'], 'L1_attn_lambda_q1': _L1_attn_in['lambda_q1'], 'L1_attn_lambda_k1': _L1_attn_in['lambda_k1'], 'L1_attn_lambda_q2': _L1_attn_in['lambda_q2'], 'L1_attn_lambda_k2': _L1_attn_in['lambda_k2'], 'L1_ffn_Wg': _L1_ffn_in['Wg'], 'L1_ffn_W1': _L1_ffn_in['W1'], 'L1_ffn_W2': _L1_ffn_in['W2']}
    _x0 = _d['L0_attn_x']
    _d['L0_attn_x'] = jax.random.normal(jax.random.fold_in(jax.random.key(seed), 1), (4, 2048, 256), dtype=_x0.dtype)
    del _x0
    return _d

def reference(L0_attn_x, L0_attn_A_log, L0_attn_W_delta, L0_attn_b_delta, L0_attn_W_B, L0_attn_W_C, L0_attn_D_skip, L0_attn_norm_weight, L0_ffn_Ws1, L0_ffn_Ws2, L0_ffn_W1, L0_ffn_W2, L0_ffn_Wr, L1_attn_Wq, L1_attn_bq, L1_attn_Wk, L1_attn_bk, L1_attn_Wv, L1_attn_bv, L1_attn_Wp, L1_attn_bp, L1_attn_lambda_q1, L1_attn_lambda_k1, L1_attn_lambda_q2, L1_attn_lambda_k2, L1_ffn_Wg, L1_ffn_W1, L1_ffn_W2):

    def _L0_attn_ref(x, A_log, W_delta, b_delta, W_B, W_C, D_skip, norm_weight):
        import jax, jax.numpy as jnp
        import numpy as np
        DT_MIN, DT_MAX, STAB_EPS, RMS_EPS = (0.0001, 10.0, 1e-08, 1e-06)

        def soft_clamp(x, mn=DT_MIN, mx=DT_MAX):
            center = (mx + mn) / 2.0
            half = (mx - mn) / 2.0
            return center + half * jnp.tanh((x - center) / half)
        rms = jnp.sqrt(jnp.mean(x * x, axis=-1, keepdims=True) + RMS_EPS)
        xn = norm_weight * x / rms
        delta = soft_clamp(jax.nn.softplus(xn @ W_delta + b_delta))
        Bp = xn @ W_B
        C = xn @ W_C
        A = -jnp.exp(A_log)
        half_dA = 0.5 * delta[..., None] * A
        denom_inv = 1.0 / jnp.maximum(1.0 - half_dA, STAB_EPS)
        A_bar = (1.0 + half_dA) * denom_inv
        B_bar = jnp.sqrt(delta)[..., None] * Bp[:, :, None, :] * denom_inv
        Bx = B_bar * xn[..., None]

        def step(h, inp):
            a_t, bx_t, c_t = inp
            h = a_t * h + bx_t
            y_t = jnp.einsum('bdn,bn->bd', h, c_t)
            return (h, y_t)
        h0 = jnp.zeros((x.shape[0], A.shape[0], A.shape[1]), x.dtype)
        seq = (jnp.moveaxis(A_bar, 1, 0), jnp.moveaxis(Bx, 1, 0), jnp.moveaxis(C, 1, 0))
        _, ys = jax.lax.scan(step, h0, seq)
        y = jnp.moveaxis(ys, 0, 1) + D_skip * xn
        return y

    def _L0_ffn_ref(x, Ws1, Ws2, W1, W2, Wr):
        import jax, jax.numpy as jnp
        import numpy as np
        D_MODEL = 256
        EXPERT_DIM = 128
        N_EXPERTS = 8
        TOP_K = 2

        def _sq_relu(h):
            return jnp.square(jax.nn.relu(h))
        shape = x.shape
        xf = x.reshape(-1, D_MODEL)
        out_shared = _sq_relu(xf @ Ws1) @ Ws2
        logits = xf @ Wr
        top_vals, top_idx = jax.lax.top_k(logits, TOP_K)
        rw = jax.nn.softmax(top_vals.astype(jnp.float32), axis=-1).astype(x.dtype)
        onehot = jax.nn.one_hot(top_idx, N_EXPERTS, dtype=x.dtype)
        prob = jnp.einsum('tk,tke->te', rw, onehot)
        prob = jnp.trunc(prob)
        h = _sq_relu(jnp.einsum('td,edf->tef', xf, W1))
        y = jnp.einsum('tef,efd->ted', h, W2)
        out_routed = jnp.einsum('ted,te->td', y, prob)
        return (out_shared + out_routed).reshape(shape)

    def _L1_attn_ref(x, Wq, bq, Wk, bk, Wv, bv, Wp, bp, lambda_q1, lambda_k1, lambda_q2, lambda_k2):
        import jax, jax.numpy as jnp
        import numpy as np
        EMBED_DIM = 256
        NUM_HEADS = 16
        EFF_HEADS = NUM_HEADS // 2
        HEAD_DIM = EMBED_DIM // NUM_HEADS
        LAMBDA_INIT = 0.8
        B, N = (2, 512)
        Bb, Nn, C = x.shape
        H, H2, hd = (NUM_HEADS, EFF_HEADS, HEAD_DIM)
        scale = hd ** (-0.5)
        q = (x @ Wq.T + bq).reshape(Bb, Nn, H, hd).transpose(0, 2, 1, 3)
        k = (x @ Wk.T + bk).reshape(Bb, Nn, H, hd).transpose(0, 2, 1, 3)
        v = (x @ Wv.T + bv).reshape(Bb, Nn, H, hd).transpose(0, 2, 1, 3)
        q1, q2 = (q[:, :H2], q[:, H2:])
        k1, k2 = (k[:, :H2], k[:, H2:])
        v1, v2 = (v[:, :H2], v[:, H2:])
        l1 = jnp.exp(jnp.minimum((lambda_q1 * lambda_k1).sum((-1, -2)), 5.0))
        l2 = jnp.exp(jnp.minimum((lambda_q2 * lambda_k2).sum((-1, -2)), 5.0))
        lv = (l1 - l2 + LAMBDA_INIT).mean()
        a1 = jax.nn.softmax(jnp.einsum('bhnd,bhmd->bhnm', q1, k1) * scale, axis=-1)
        x1 = jnp.einsum('bhnm,bhmd->bhnd', a1, v1).transpose(0, 2, 1, 3).reshape(Bb, Nn, C // 2)
        a2 = jax.nn.softmax(jnp.einsum('bhnd,bhmd->bhnm', q2, k2) * scale, axis=-1)
        x2 = jnp.einsum('bhnm,bhmd->bhnd', a2, v2).transpose(0, 2, 1, 3).reshape(Bb, Nn, C // 2)
        out = jnp.concatenate([x1 - lv * x2, x2], axis=-1) @ Wp.T + bp
        return out

    def _L1_ffn_ref(hidden_states, Wg, W1, W2):
        import jax, jax.numpy as jnp
        import numpy as np
        B, C, D = (2, 512, 256)
        I = 512
        E, K = (8, 2)
        CF = 1.25
        Bx, Cx, d = hidden_states.shape
        N = Bx * Cx
        cap = int(N * K * CF / E)
        x = hidden_states.reshape(N, d)
        logits = x @ Wg.T
        top_v, top_i = jax.lax.top_k(logits, K)
        gates = jax.nn.softmax(top_v, axis=-1)
        flat_e = top_i.reshape(N * K)
        gates_f = gates.reshape(N * K)
        tok = jnp.repeat(jnp.arange(N), K)
        onehot = jax.nn.one_hot(flat_e, E, dtype=jnp.int32)
        pos = jnp.cumsum(onehot, axis=0) - 1
        pos_f = jnp.take_along_axis(pos, flat_e[:, None], axis=1)[:, 0]
        keep = pos_f < cap
        pos_safe = jnp.where(keep, pos_f, cap)
        exp_batches = jnp.zeros((E, cap, d), x.dtype).at[flat_e, pos_safe].set(x[tok], mode='drop')
        h = jnp.einsum('ecd,edf->ecf', exp_batches, W1)
        inp, gate = jnp.split(h, 2, axis=-1)
        h = jax.nn.gelu(inp, approximate=False) * gate
        exp_out = jnp.einsum('eci,eid->ecd', h, W2)
        gathered = exp_out[flat_e, jnp.minimum(pos_safe, cap - 1)]
        contrib = jnp.where(keep, gates_f, 0.0)[:, None] * gathered
        out = jax.ops.segment_sum(contrib, tok, num_segments=N)
        return out.reshape(Bx, Cx, d)
    x = L0_attn_x
    xn = _layernorm(x, axis=-1)
    s = _L0_attn_ref(xn, L0_attn_A_log, L0_attn_W_delta, L0_attn_b_delta, L0_attn_W_B, L0_attn_W_C, L0_attn_D_skip, L0_attn_norm_weight)
    g = _silu(_L0_ffn_ref(xn, L0_ffn_Ws1, L0_ffn_Ws2, L0_ffn_W1, L0_ffn_W2, L0_ffn_Wr))
    x = x + s * g
    xn = _layernorm(x, axis=-1)
    s = _L1_attn_ref(xn, L1_attn_Wq, L1_attn_bq, L1_attn_Wk, L1_attn_bk, L1_attn_Wv, L1_attn_bv, L1_attn_Wp, L1_attn_bp, L1_attn_lambda_q1, L1_attn_lambda_k1, L1_attn_lambda_q2, L1_attn_lambda_k2)
    g = _silu(_L1_ffn_ref(xn, L1_ffn_Wg, L1_ffn_W1, L1_ffn_W2))
    x = x + s * g
    return x

_drawn_inputs = setup_inputs


def setup_inputs(seed=0):
    import zlib

    import numpy as np

    out = dict(_drawn_inputs(seed))
    spreads = {'L0_attn_norm_weight': (1.0, 0.6),
     'L1_attn_bq': (0.0, 0.8),
     'L1_attn_bk': (0.0, 2.0),
     'L1_attn_bv': (0.0, 0.8),
     'L1_attn_bp': (0.0, 0.8)}
    factors = {'L0_attn_A_log': 4.697,
     'L0_attn_W_delta': 8.0,
     'L0_attn_b_delta': 8.0,
     'L0_attn_W_B': 2.945,
     'L0_attn_W_C': 2.91,
     'L0_attn_D_skip': 8.0,
     'L1_attn_Wq': 8.0,
     'L1_attn_Wk': 8.0,
     'L1_attn_Wv': 8.0,
     'L1_attn_Wp': 8.0,
     'L1_attn_lambda_q1': 21.831,
     'L1_attn_lambda_k1': 8.0,
     'L1_attn_lambda_q2': 8.0,
     'L1_attn_lambda_k2': 64.0,
     'L1_ffn_Wg': 8.0,
     'L1_ffn_W1': 8.0,
     'L1_ffn_W2': 8.0}
    for name, (base, spread) in spreads.items():
        noise = np.random.default_rng([zlib.crc32(name.encode()), seed]).standard_normal(out[name].shape)
        drawn = base * np.exp(spread * noise) if base else spread * noise
        out[name] = jnp.asarray(drawn.astype(out[name].dtype))
    for name, factor in factors.items():
        out[name] = (out[name] * factor).astype(out[name].dtype)
    return out
```

```python
import numpy as np
import concourse.bass as bass
from concourse import mybir
from contextlib import ExitStack
from collections import namedtuple

F32 = mybir.dt.float32
BF16 = mybir.dt.bfloat16
I32 = mybir.dt.int32
U32 = mybir.dt.uint32
ALU = mybir.AluOpType
ACT = mybir.ActivationFunctionType
AX_X = mybir.AxisListType.X

P = 128
B, L, D = 4, 2048, 256
NS = 16
T = B * L
KD = D // P
TILES = L // P
HALF = L // 2
BANK = 512
DT_MIN, DT_MAX, RMS_EPS, LN_EPS = 0.0001, 10.0, 1e-06, 1e-05
CENTER, HALFSPAN = (DT_MAX + DT_MIN) / 2.0, (DT_MAX - DT_MIN) / 2.0
LN2 = 0.6931471805599453
E0, F0 = 8, 128


def named(**parts):
    return namedtuple("Parts", parts)(**parts)


def stage_sems(nc, ctx, stage, names):
    found = {n: ctx.enter_context(nc.semaphore(f"{stage}_{n}")) for n in names.split()}

    def clear():
        nums = sorted(x.num for x in found.values())
        first = nums[0]
        for n, after in zip(nums, nums[1:] + [None]):
            if after != n + 1:
                nc.sync.sem_clear(range(first, n + 1))
                first = after
        nc.all_engine_barrier()

    return named(clear=clear, **found)


def prepare_batch(nc, b, io, m):
    with ExitStack() as ctx:
        s = stage_sems(nc, ctx, "prepare_batch", "x_in stats mv root rstd ms root2 rr x0 xr turned evac_a evac_d z zb t_abs t_exp t_ln sp th delta lnd sq u bc bcx p1 r1 p2 r2")
        x0, xr = m.nat, m.work[:, 0:4096].rearrange("p (i d) -> p i d", i=TILES)
        t1 = m.work[:, 4096:8192].rearrange("p (k t) -> p k t", k=KD)
        bcx, r1 = m.work[0:96, 8192:10240], m.work[0:96, 10240:12288]
        p2 = m.work[0:96, 12288:13312].bitcast(BF16)
        stats, mv, sm = m.stats, m.mv, m.small
        with nc.Block() as block:

            @block.sync
            def _(sp):
                sp.dma_start(m.x[:], io.x[bass.ts(b, 1), :, :].rearrange("o (i p) d -> p (o i) d", p=P)).then_inc(s.x_in, 16)

            @block.vector
            def _(dve):
                dve.wait_ge(s.x_in, 16)
                for i in range(TILES):
                    dve.bn_stats(stats[:, i, :], m.x[:, i, :]).then_inc(s.stats, 1)
                for i in range(TILES):
                    dve.wait_ge(s.stats, i + 1)
                    dve.bn_aggr(mv[:, i, :], stats[:, i, :]).then_inc(s.mv, 1)
                dve.wait_ge(s.root, 1)
                dve.reciprocal(sm[:, 1, :], sm[:, 0, :]).then_inc(s.rstd, 1)
                dve.wait_ge(s.rstd, 1)
                dve.tensor_tensor(sm[:, 2, :], sm[:, 1, :], sm[:, 1, :], ALU.mult).then_inc(s.ms, 1)
                dve.wait_ge(s.ms, 1)
                dve.wait_ge(s.mv, TILES)
                dve.tensor_tensor(sm[:, 3, :], sm[:, 2, :], mv[:, :, 1], ALU.mult).then_inc(s.ms, 1)
                dve.wait_ge(s.root2, 1)
                dve.reciprocal(sm[:, 5, :], sm[:, 4, :]).then_inc(s.rr, 1)
                for i in range(TILES):
                    dve.tensor_scalar(x0[:, i, :], m.x[:, i, :], mv[:, i, 0:1], sm[:, 1, i:i + 1],
                                      ALU.subtract, ALU.mult).then_inc(s.x0, 1)
                dve.wait_ge(s.rr, 1)
                for i in range(TILES):
                    dve.wait_ge(s.x0, i + 1)
                    dve.tensor_scalar(xr[:, i, :], x0[:, i, :], sm[:, 5, i:i + 1], None, ALU.mult).then_inc(s.xr, 1)
                for g in range(4):
                    for k in range(KD):
                        dve.wait_ge(s.turned, 8 + g * KD + k + 1)
                        dve.tensor_scalar(m.xrT[:, k, bass.ts(g, BANK)], m.bank[g * KD + k][:, :], m.nw[:, k:k + 1],
                                          None, ALU.mult).then_inc(s.evac_d, 1)
                dve.wait_ge(s.t_ln, 1)
                dve.scalar_tensor_tensor(m.lnd[:], m.lnd[:], 0.0, t1, ALU.max, ALU.add).then_inc(s.sp, 1)
                dve.wait_ge(s.th, 1)
                dve.tensor_scalar(m.lnd[:], m.lnd[:], HALFSPAN, CENTER, ALU.mult, ALU.add).then_inc(s.delta, 1)
                dve.wait_ge(s.p1, 1)
                dve.tensor_tensor(r1, bcx, m.bc3[:], ALU.subtract).then_inc(s.r1, 1)
                dve.wait_ge(s.sq, 1)
                dve.tensor_tensor(m.u[:], t1, m.xrT[:], ALU.mult).then_inc(s.u, 1)
                dve.wait_ge(s.p2, 1)
                dve.tensor_tensor(bcx, r1, p2, ALU.subtract).then_inc(s.r2, 1)
                dve.wait_ge(s.r1, 1)
                dve.tensor_copy(m.bc3[32:64, :], r1[32:64, :]).then_inc(s.r2, 1)
                dve.wait_ge(s.r2, 2)
                dve.tensor_copy(m.bc3[64:96, :], bcx[64:96, :]).then_inc(s.r2, 1)

            @block.scalar
            def _(act):
                act.wait_ge(s.mv, TILES)
                act.activation(sm[:, 0, :], mv[:, :, 1], ACT.Sqrt, bias=m.eps[:, 0:1]).then_inc(s.root, 1)
                act.wait_ge(s.ms, 2)
                act.activation(sm[:, 4, :], sm[:, 3, :], ACT.Sqrt, bias=m.eps[:, 1:2]).then_inc(s.root2, 1)
                for g in range(4):
                    for k in range(KD):
                        act.wait_ge(s.turned, g * KD + k + 1)
                        act.copy(m.x0T[:, k, bass.ts(g, BANK)], m.bank[g * KD + k][:, :]).then_inc(s.evac_a, 1)
                for j in range(8):
                    k, g = j // 4, j % 4
                    act.wait_ge(s.z, j + 1)
                    act.activation(m.lnd[:, k, bass.ts(g, BANK)], m.bank[j][:, :], ACT.Identity,
                                   bias=m.bd[:, k:k + 1]).then_inc(s.zb, 1)
                act.wait_ge(s.zb, 8)
                act.activation(t1, m.lnd[:], ACT.Abs).then_inc(s.t_abs, 1)
                act.wait_ge(s.t_abs, 1)
                act.activation(t1, t1, ACT.Exp, scale=-1.0).then_inc(s.t_exp, 1)
                act.wait_ge(s.t_exp, 1)
                act.activation(t1, t1, ACT.Ln, bias=1.0).then_inc(s.t_ln, 1)
                for g in range(4):
                    act.wait_ge(s.bc, g + 1)
                    act.copy(bcx[:, bass.ts(g, BANK)], m.bank[g][0:96, :]).then_inc(s.bcx, 1)
                act.wait_ge(s.bcx, 4)
                act.copy(m.bc3[:], bcx).then_inc(s.p1, 1)
                act.wait_ge(s.sp, 1)
                act.activation(m.lnd[:], m.lnd[:], ACT.Tanh, scale=1.0 / HALFSPAN, bias=m.eps[:, 2:3]).then_inc(s.th, 1)
                act.wait_ge(s.r1, 1)
                act.copy(p2, r1).then_inc(s.p2, 1)
                act.wait_ge(s.delta, 1)
                act.activation(m.lnd[:], m.lnd[:], ACT.Ln).then_inc(s.lnd, 1)
                act.wait_ge(s.lnd, 1)
                act.activation(t1, m.lnd[:], ACT.Exp, scale=0.5).then_inc(s.sq, 1)

            @block.tensor
            def _(pe):
                for which, src, ready in ((0, x0, s.x0), (1, xr, s.xr)):
                    for g in range(4):
                        pe.wait_ge(ready, 4 * g + 4)
                        for k in range(KD):
                            if which:
                                pe.wait_ge(s.evac_a, g * KD + k + 1)
                            for q in range(4):
                                t = pe.transpose(m.bank[g * KD + k][:, bass.ts(q, P)], src[:, 4 * g + q, bass.ts(k, P)], m.ident[:])
                            t.then_inc(s.turned, 1)
                for j in range(8):
                    k, g = j // 4, j % 4
                    pe.wait_ge(s.evac_d, 8)
                    for c in range(KD):
                        mm = pe.matmul(m.bank[j][:, :], m.wd[:, c, bass.ts(k, P)], m.xrT[:, c, bass.ts(g, BANK)],
                                       start=(c == 0), stop=(c == KD - 1))
                    mm.then_inc(s.z, 1)
                for g in range(4):
                    pe.wait_ge(s.zb, g + 1)
                    for c in range(KD):
                        mm = pe.matmul(m.bank[g][0:96, :], m.wbc[:, c, :], m.xrT[:, c, bass.ts(g, BANK)],
                                       start=(c == 0), stop=(c == KD - 1))
                    mm.then_inc(s.bc, 1)
        s.clear()


def scan_half(nc, half, m):
    with ExitStack() as ctx:
        s = stage_sems(nc, ctx, f"scan{half}", "bc_psum bc_sbuf inv decay w bx h hc y_added carried y_open y_out")
        work = lambda n: m.work[:, bass.ts(n, HALF)]
        Bs, Cs = [work(0), work(1)], [work(2), work(3)]
        inv, dec, w, bx, h, hc = ([work(4 + 2 * n), work(5 + 2 * n)] for n in range(6))
        y = [m.pair[0], m.pair[1]]
        pB, pC = m.pair[2], m.pair[3]
        t0 = half * HALF
        last = NS - 1
        with nc.Block() as block:

            @block.tensor
            def _(pe):
                for k in range(KD):
                    for q in range(2):
                        mm = pe.matmul(y[k][:, q, :], m.dskip[:, k, :], m.xrT[:, k, t0 + BANK * q:t0 + BANK * (q + 1)],
                                       start=True, stop=True)
                mm.then_inc(s.y_open, 1)

                def spread(n, it):
                    pe.wait_ge(s.bc_sbuf, 2 * it)
                    for dst, row in ((pB, n), (pC, n + NS)):
                        for q in range(2):
                            mm = pe.matmul(dst[:, q, :], m.sel[:, bass.ts(row, P)], m.bc3[:, t0 + BANK * q:t0 + BANK * (q + 1)],
                                           start=True, stop=True)
                        mm.then_inc(s.bc_psum, 1)

                def add(it):
                    for k in range(KD):
                        pe.wait_ge(s.hc, 2 * it + k + 1)
                        for q in range(2):
                            mm = pe.matmul(y[k][:, q, :], m.ident[:], hc[k][:, bass.ts(q, BANK)],
                                           start=False, stop=True, skip_group_check=True)
                        mm.then_inc(s.y_added, 1)

                for dst, row in ((pB, 0), (pC, NS)):
                    for q in range(2):
                        mm = pe.matmul(dst[:, q, :], m.sel[:, bass.ts(row, P)], m.bc3[:, t0 + BANK * q:t0 + BANK * (q + 1)],
                                       start=True, stop=True)
                    mm.then_inc(s.bc_psum, 1)
                spread(1, 1)
                with pe.Fori(0, NS - 2) as n:
                    spread(n + 2, n + 2)
                    add(n)
                add(NS - 2)
                add(NS - 1)

            @block.scalar
            def _(act):
                def bc_out(it, j):
                    act.wait_ge(s.bc_psum, 2 * it + 1)
                    act.wait_ge(s.w, 2 * it - 2)
                    act.copy(Bs[j], pB[:].rearrange("p a b -> p (a b)")).then_inc(s.bc_sbuf, 1)
                    act.wait_ge(s.bc_psum, 2 * it + 2)
                    act.wait_ge(s.hc, 2 * it - 2)
                    act.copy(Cs[j], pC[:].rearrange("p a b -> p (a b)")).then_inc(s.bc_sbuf, 1)

                def decays(n, it, first=False):
                    for k in range(KD):
                        if not first:
                            act.wait_ge(s.bx, 2 * it - 1 + k)
                        act.activation(inv[k], m.lnd[:, k, t0:t0 + HALF], ACT.Sigmoid, scale=-1.0,
                                       bias=m.ainv[:, k, bass.ds(n, 1)]).then_inc(s.inv, 1)
                        if not first:
                            act.wait_ge(s.h, 2 * it - 1 + k)
                        act.activation(dec[k], m.lnd[:, k, t0:t0 + HALF], ACT.Tanh, scale=-0.5,
                                       bias=m.adec[:, k, bass.ds(n, 1)]).then_inc(s.decay, 1)

                for it in range(2):
                    act.wait_ge(s.bc_psum, 2 * it + 1)
                    act.copy(Bs[it], pB[:].rearrange("p a b -> p (a b)")).then_inc(s.bc_sbuf, 1)
                    act.wait_ge(s.bc_psum, 2 * it + 2)
                    act.copy(Cs[it], pC[:].rearrange("p a b -> p (a b)")).then_inc(s.bc_sbuf, 1)
                    decays(it, it, first=(it == 0))
                with act.Fori(1, NS // 2) as pair:
                    for j in range(2):
                        bc_out(2 * pair + j, j)
                        decays(2 * pair + j, 2 * pair + j)
                act.wait_ge(s.y_added, 2 * NS)
                for k in range(KD):
                    act.copy(m.sT[:, k, t0:t0 + HALF], y[k][:].rearrange("p a b -> p (a b)")).then_inc(s.y_out, 1)

            @block.gpsimd
            def _(pool):
                def inputs(it, j, first=False):
                    for k in range(KD):
                        pool.wait_ge(s.bc_sbuf, 2 * it + 1)
                        if not first:
                            pool.wait_ge(s.bx, 2 * it - 1 + k)
                        pool.tensor_tensor(w[k], m.u[:, k, t0:t0 + HALF], Bs[j], ALU.mult).then_inc(s.w, 1)

                def carry(n, it):
                    if half:
                        return
                    for k in range(KD):
                        pool.wait_ge(s.h, 2 * it + k + 1)
                        pool.tensor_copy(m.carry[:, k, bass.ds(n, 1)], h[k][:, HALF - 1:HALF]).then_inc(s.carried, 1)

                inputs(0, 0, first=True)
                inputs(1, 1)
                carry(0, 0)
                with pool.Fori(1, NS // 2) as pair:
                    for j in range(2):
                        it = 2 * pair + j
                        inputs(it, j)
                        carry(it - 1, it - 1)
                carry(last, last)

            @block.vector
            def _(dve):
                def step(n, it, j, first=False):
                    for k in range(KD):
                        dve.wait_ge(s.inv, 2 * it + k + 1)
                        dve.wait_ge(s.w, 2 * it + k + 1)
                        if not first:
                            dve.wait_ge(s.h, 2 * it - 1 + k)
                        dve.tensor_tensor(bx[k], w[k], inv[k], ALU.mult).then_inc(s.bx, 1)
                    for k in range(KD):
                        dve.wait_ge(s.bx, 2 * it + k + 1)
                        dve.wait_ge(s.decay, 2 * it + k + 1)
                        if not first:
                            dve.wait_ge(s.hc, 2 * it - 1 + k)
                            if not half:
                                dve.wait_ge(s.carried, 2 * it - 1 + k)
                        dve.tensor_tensor_scan(h[k], dec[k], bx[k], m.carry[:, k, bass.ds(n, 1)] if half else 0.0,
                                               ALU.mult, ALU.add).then_inc(s.h, 1)
                    for k in range(KD):
                        dve.wait_ge(s.h, 2 * it + k + 1)
                        dve.wait_ge(s.bc_sbuf, 2 * it + 2)
                        if not first:
                            dve.wait_ge(s.y_added, 2 * it - 1 + k)
                        dve.tensor_tensor(hc[k], h[k], Cs[j], ALU.mult).then_inc(s.hc, 1)

                step(0, 0, 0, first=True)
                step(1, 1, 1)
                with dve.Fori(1, NS // 2) as pair:
                    for j in range(2):
                        step(2 * pair + j, 2 * pair + j, j)
        s.clear()


def first_ffn(nc, e, m, op):
    with ExitStack() as ctx:
        s = stage_sems(nc, ctx, f"ffn_{op}", "hid relu sq out acc")
        relu = [m.work[:, bass.ts(n, BANK)] for n in range(4)]
        sq = [m.work[:, bass.ts(n, BANK)] for n in range(4, 8)]
        with nc.Block() as block:

            @block.tensor
            def _(pe):
                for g in range(4):
                    for c in range(KD):
                        mm = pe.matmul(m.bank[g][:, :], m.w1[:, c, :], m.x0T[:, c, bass.ts(g, BANK)],
                                       start=(c == 0), stop=(c == KD - 1))
                    mm.then_inc(s.hid, 1)
                for i in range(TILES):
                    pe.wait_ge(s.sq, i // 4 + 1)
                    if i >= 4:
                        pe.wait_ge(s.acc, i - 3)
                    pe.matmul(m.bank[4 + i % 4][:, 0:D], sq[i // 4][:, bass.ts(i % 4, P)], m.w2[:],
                              start=True, stop=True).then_inc(s.out, 1)

            @block.scalar
            def _(act):
                for g in range(4):
                    act.wait_ge(s.hid, g + 1)
                    act.activation(relu[g], m.bank[g][:, :], ACT.Relu).then_inc(s.relu, 1)
                    act.wait_ge(s.relu, g + 1)
                    act.activation(sq[g], relu[g], ACT.Square).then_inc(s.sq, 1)

            @block.vector
            def _(dve):
                for i in range(TILES):
                    dve.wait_ge(s.out, i + 1)
                    if op == "first":
                        dve.tensor_copy(m.nat[:, i, :], m.bank[4 + i % 4][:, 0:D]).then_inc(s.acc, 1)
                    else:
                        dve.scalar_tensor_tensor(m.nat[:, i, :], m.bank[4 + i % 4][:, 0:D], m.prob[:, i, bass.ds(e, 1)],
                                                 m.nat[:, i, :], ALU.mult, ALU.add).then_inc(s.acc, 1)
        s.clear()


def first_router(nc, m):
    with ExitStack() as ctx:
        s = stage_sems(nc, ctx, "first_router", "logit top diff ex s1 s2 prob pmax count flag")
        lg, top, t = m.lg, m.top, m.small
        with nc.Block() as block:

            @block.tensor
            def _(pe):
                for i in range(TILES):
                    for c in range(KD):
                        mm = pe.matmul(m.bank[0][:, bass.ts(i, E0)], m.x0T[:, c, bass.ts(i, P)], m.wr[:, c, :],
                                       start=(c == 0), stop=(c == KD - 1))
                mm.then_inc(s.logit, 1)
                pe.wait_ge(s.pmax, 1)
                pe.matmul(m.bank[1][0:1, 0:1], m.pmax, m.ones[:, 0:1], start=True, stop=True).then_inc(s.count, 1)

            @block.vector
            def _(dve):
                dve.wait_ge(s.logit, 1)
                dve.tensor_copy(lg[:].rearrange("p i e -> p (i e)"), m.bank[0][:, 0:TILES * E0]).then_inc(s.top, 1)
                dve.wait_ge(s.top, 1)
                for i in range(TILES):
                    dve.max(top[:, i, :], lg[:, i, :]).then_inc(s.top, 1)
                dve.wait_ge(s.top, 1 + TILES)
                dve.tensor_tensor(t[:, 0, :], top[:, :, 1], top[:, :, 0], ALU.subtract).then_inc(s.diff, 1)
                dve.wait_ge(s.ex, 1)
                dve.tensor_scalar(t[:, 2, :], t[:, 1, :], 1.0, None, ALU.add).then_inc(s.s1, 1)
                dve.wait_ge(s.s1, 1)
                dve.tensor_scalar(t[:, 3, :], t[:, 2, :], 1.0, None, ALU.is_equal).then_inc(s.s2, 1)
                for i in range(TILES):
                    dve.wait_ge(s.s2, 1)
                    dve.tensor_scalar(m.prob[:, i, :], lg[:, i, :], top[:, i, 0:1], t[:, 3, i:i + 1],
                                      ALU.is_equal, ALU.mult).then_inc(s.prob, 1)
                dve.wait_ge(s.prob, TILES)
                dve.tensor_reduce(m.pmax, m.prob.rearrange("p i e -> p (i e)"), AX_X, ALU.max).then_inc(s.pmax, 1)
                dve.wait_ge(s.count, 1)
                dve.tensor_copy(m.taken, m.bank[1][0:1, 0:1]).then_inc(s.flag, 1)

            @block.scalar
            def _(act):
                act.wait_ge(s.diff, 1)
                act.activation(t[:, 1, :], t[:, 0, :], ACT.Exp).then_inc(s.ex, 1)
        s.clear()


def load_expert(nc, w1, w2, m, op):
    with ExitStack() as ctx:
        s = stage_sems(nc, ctx, f"load_{op}", "w_in")
        with nc.Block() as block:

            @block.sync
            def _(sp):
                sp.dma_start(m.w1[:], w1.rearrange("(c p) f -> p c f", p=P)).then_inc(s.w_in, 16)
                sp.dma_start(m.w2[:], w2).then_inc(s.w_in, 16)
                sp.wait_ge(s.w_in, 32)
        s.clear()


def finish_batch(nc, b, io, m):
    with ExitStack() as ctx:
        s = stage_sems(nc, ctx, "finish_batch", "x_in turned sig silu g x1 stats mv root rstd xn x1_out xn_out turned2 evac stored x_used")
        sig = m.work[:, 0:4096].rearrange("p (i d) -> p i d", i=TILES)
        xn = m.work[:, 4096:8192].rearrange("p (i d) -> p i d", i=TILES)
        stats, mv, sm = m.stats, m.mv, m.small
        with nc.Block() as block:

            @block.scalar
            def _(act):
                act.activation(sig, m.nat[:], ACT.Sigmoid).then_inc(s.sig, 1)
                act.wait_ge(s.mv, TILES)
                act.activation(sm[:, 0, :], mv[:, :, 1], ACT.Sqrt, bias=m.eps[:, 0:1]).then_inc(s.root, 1)
                for g in range(4):
                    for k in range(KD):
                        act.wait_ge(s.turned2, g * KD + k + 1)
                        act.copy(m.x0T[:, k, bass.ts(g, BANK)], m.bank[g * KD + k][:, :]).then_inc(s.evac, 1)

            @block.tensor
            def _(pe):
                for i in range(TILES):
                    if i >= 8:
                        pe.wait_ge(s.g, i - 7)
                    for k in range(KD):
                        t = pe.transpose(m.bank[i % 8][:, bass.ts(k, P)], m.sT[:, k, bass.ts(i, P)], m.ident[:])
                    t.then_inc(s.turned, 1)
                for g in range(4):
                    pe.wait_ge(s.xn, 4 * g + 4)
                    for k in range(KD):
                        pe.wait_ge(s.g, TILES)
                        for q in range(4):
                            t = pe.transpose(m.bank[g * KD + k][:, bass.ts(q, P)], xn[:, 4 * g + q, bass.ts(k, P)], m.ident[:])
                        t.then_inc(s.turned2, 1)

            @block.vector
            def _(dve):
                dve.wait_ge(s.sig, 1)
                dve.tensor_tensor(sig, sig, m.nat[:], ALU.mult).then_inc(s.silu, 1)
                dve.wait_ge(s.silu, 1)
                for i in range(TILES):
                    dve.wait_ge(s.turned, i + 1)
                    dve.tensor_tensor(sig[:, i, :], sig[:, i, :], m.bank[i % 8][:, 0:D], ALU.mult).then_inc(s.g, 1)
                for i in range(TILES):
                    dve.wait_ge(s.g, i + 1)
                    dve.tensor_tensor(m.x[:, i, :], m.x[:, i, :], sig[:, i, :], ALU.add).then_inc(s.x1, 1)
                for i in range(TILES):
                    dve.wait_ge(s.x1, i + 1)
                    dve.bn_stats(stats[:, i, :], m.x[:, i, :]).then_inc(s.stats, 1)
                for i in range(TILES):
                    dve.wait_ge(s.stats, i + 1)
                    dve.bn_aggr(mv[:, i, :], stats[:, i, :]).then_inc(s.mv, 1)
                dve.wait_ge(s.root, 1)
                dve.reciprocal(sm[:, 1, :], sm[:, 0, :]).then_inc(s.rstd, 1)
                dve.wait_ge(s.rstd, 1)
                for i in range(TILES):
                    dve.tensor_scalar(xn[:, i, :], m.x[:, i, :], mv[:, i, 0:1], sm[:, 1, i:i + 1],
                                      ALU.subtract, ALU.mult).then_inc(s.xn, 1)

            @block.sync
            def _(sp):
                sp.wait_ge(s.x1, TILES)
                sp.dma_start(io.x1[bass.ts(b, 1), :, :].rearrange("o (i p) d -> p (o i) d", p=P), m.x[:]).then_inc(s.stored, 16)
                sp.wait_ge(s.xn, TILES)
                sp.dma_start(io.xn[bass.ts(b, 1), :, :].rearrange("o (i p) d -> p (o i) d", p=P), xn).then_inc(s.stored, 16)
                sp.wait_ge(s.evac, 8)
                for k in range(KD):
                    sp.dma_start(io.xnT[bass.ts(b, 1), k, :, :].rearrange("o p t -> p (o t)"), m.x0T[:, k, :]).then_inc(s.stored, 16)
                sp.wait_ge(s.stored, 64)
        s.clear()


def build_first_layer(nc, io):
    with ExitStack() as ctx:
        t = {}

        def sb(name, shape, dt=F32):
            made = ctx.enter_context(nc.sbuf_tensor("l0_" + name, shape, dt))
            t[name] = made[:]
        sb("x", [P, TILES, D])
        sb("nat", [P, TILES, D])
        sb("x0T", [P, KD, L])
        sb("xrT", [P, KD, L])
        sb("lnd", [P, KD, L])
        sb("u", [P, KD, L])
        sb("sT", [P, KD, L])
        sb("work", [P, 16 * HALF])
        sb("bc3", [96, L], BF16)
        sb("sel", [96, 2 * NS * P], BF16)
        sb("ident", [P, P])
        sb("dskip", [P, KD, P])
        sb("wd", [P, KD, D])
        sb("wbc", [P, KD, 96])
        sb("wr", [P, KD, E0])
        sb("w1", [P, KD, F0])
        sb("w2", [P, D])
        sb("nw", [P, KD]); sb("bd", [P, KD]); sb("ds", [P, KD])
        sb("alog", [P, KD, NS]); sb("ainv", [P, KD, NS]); sb("adec", [P, KD, NS])
        sb("carry", [P, KD, NS])
        sb("stats", [P, TILES, 6]); sb("mv", [P, TILES, 2]); sb("small", [P, 6, TILES])
        sb("lg", [P, TILES, E0]); sb("top", [P, TILES, 8]); sb("prob", [P, TILES, E0])
        sb("eps", [P, 4]); sb("ones", [P, P]); sb("pmax", [P, 1]); sb("taken", [1, 1], I32)
        m = named(**t)
        s = stage_sems(nc, ctx, "build_first_layer", "w_in const_ready")
        with ExitStack() as c2:
            with nc.Block() as block:

                @block.sync
                def _(sp):
                    cols = [(m.wd, io.W_delta.rearrange("(c p) n -> p c n", p=P)), (m.wr, io.Wr.rearrange("(c p) n -> p c n", p=P)),
                            (m.alog, io.A_log.rearrange("(c p) n -> p c n", p=P)), (m.ident, io.ident), (m.sel, io.sel)]
                    for r in range(3):
                        cols.append((m.wbc[:, :, 32 * r:32 * r + NS], io.W_B.rearrange("(c p) n -> p c n", p=P)))
                        cols.append((m.wbc[:, :, 32 * r + NS:32 * r + 32], io.W_C.rearrange("(c p) n -> p c n", p=P)))
                    with nc.allow_non_contiguous_dma(reason="three columns of 128 numbers"):
                        for t, v in ((m.nw, io.norm_weight), (m.bd, io.b_delta), (m.ds, io.D_skip)):
                            sp.dma_start(t, v.rearrange("(c p) -> p c", p=P)).then_inc(s.w_in, 16)
                        for t, v in cols:
                            sp.dma_start(t, v).then_inc(s.w_in, 16)
                    sp.wait_ge(s.w_in, 16 * (3 + len(cols)))

                @block.vector
                def _(dve):
                    dve.memset(m.ones, 1.0)
                    dve.memset(m.eps[:, 0:1], LN_EPS)
                    dve.memset(m.eps[:, 1:2], RMS_EPS)
                    dve.memset(m.eps[:, 2:3], -CENTER / HALFSPAN)
                    dve.wait_ge(s.w_in, 16 * 14)
                    for k in range(KD):
                        dve.tensor_scalar(m.dskip[:, k, :], m.ident[:], m.ds[:, k:k + 1], None, ALU.mult)
                    dve.tensor_scalar(m.ainv[:], m.alog[:], -1.0, LN2, ALU.mult, ALU.add)
                    dve.tensor_scalar(m.adec[:], m.alog[:], -0.5, LN2 / 2, ALU.mult, ALU.add)
        s.clear()
        ps = ctx.enter_context(nc.psum_tensor("l0_ps", [P, 8, BANK], F32))
        t["bank"] = [ps[:, i, :] for i in range(8)]
        t["pair"] = [ps[:, 2 * i:2 * i + 2, :] for i in range(4)]
        m = named(**t)
        with nc.Fori(0, B) as b:
            prepare_batch(nc, b, io, m)
            scan_half(nc, 0, m)
            scan_half(nc, 1, m)
            first_router(nc, m)
            load_expert(nc, io.Ws1, io.Ws2, m, "first")
            first_ffn(nc, 0, m, "first")
            taken = nc.values_load(m.taken, min_val=0, max_val=P)
            with nc.If(taken > 0):
                with nc.Fori(0, E0) as e:
                    load_expert(nc, io.W1[bass.ts(e, 1), :, :].rearrange("o d f -> (o d) f"),
                                io.W2[bass.ts(e, 1), :, :].rearrange("o f d -> (o f) d"), m, "routed")
                    first_ffn(nc, e, m, "routed")
            finish_batch(nc, b, io, m)



E1, I1 = 8, 512
CAP = int(T * 2 * 1.25 / E1)
SLOTS = E1 * CAP
ROWS = 512
BLOCKS = CAP // ROWS
FAR = float(1 << 20)


def route_batch(nc, b, io, m):
    with ExitStack() as ctx:
        s = stage_sems(nc, ctx, "route", "x_in logit lg top idx chain counts base_ok gates kept")
        lg, top, idx, fidx = m.lg, m.top, m.idx, m.fidx
        oh, pos, base, tmp = m.oh, m.pos, m.base, m.tmp
        with nc.Block() as block:

            @block.sync
            def _(sp):
                for k in range(KD):
                    sp.dma_start(m.xT[:, k, :], io.xnT[bass.ts(b, 1), k, :, :].rearrange("o p t -> p (o t)")).then_inc(s.x_in, 16)
                sp.dma_start(m.xn, io.xn[bass.ts(b, 1), :, :].rearrange("o (i p) d -> p (o i) d", p=P)).then_inc(s.x_in, 16)
                sp.wait_ge(s.gates, 4)
                sp.dma_start(io.places[bass.ts(b, 1), :, :, :].rearrange("o p k i -> (o p) k i"), m.gidx).then_inc(s.kept, 16)
                sp.dma_start(io.gates[bass.ts(b, 1), :, :, :].rearrange("o p k i -> (o p) k i"), m.gate).then_inc(s.kept, 16)
                sp.wait_ge(s.kept, 32)

            @block.tensor
            def _(pe):
                pe.wait_ge(s.x_in, 48)
                for i in range(TILES):
                    for c in range(KD):
                        mm = pe.matmul(m.bank[0][:, bass.ts(i, E1)], m.xT[:, c, bass.ts(i, P)], m.wg[:, c, :],
                                       start=(c == 0), stop=(c == KD - 1))
                mm.then_inc(s.logit, 1)
                pe.wait_ge(s.chain, 3)
                pe.matmul(m.bank[1][:, 0:TILES * E1], m.before, oh[:, 2, :, :].rearrange("p i e -> p (i e)"), start=True, stop=True)
                pe.matmul(m.bank[2][:, 0:TILES * E1], m.ones, oh[:, 2, :, :].rearrange("p i e -> p (i e)"), start=True, stop=True).then_inc(s.counts, 1)

            @block.vector
            def _(dve):
                n = [0]

                def then(ins):
                    n[0] += 1
                    ins.then_inc(s.chain, 1)
                    dve.wait_ge(s.chain, n[0])

                dve.wait_ge(s.logit, 1)
                dve.tensor_copy(lg.rearrange("p i e -> p (i e)"), m.bank[0][:, 0:TILES * E1]).then_inc(s.lg, 1)
                dve.wait_ge(s.lg, 1)
                for i in range(TILES):
                    dve.max(top[:, i, :], lg[:, i, :]).then_inc(s.top, 1)
                for i in range(TILES):
                    dve.wait_ge(s.top, i + 1)
                    dve.max_index(idx[:, i, :], top[:, i, :], lg[:, i, :]).then_inc(s.idx, 1)
                dve.wait_ge(s.idx, TILES)
                for k in range(2):
                    dve.tensor_copy(fidx[:, k, :], idx[:, :, k]).then_inc(s.lg, 1)
                dve.wait_ge(s.lg, 3)
                for k in range(2):
                    then(dve.tensor_tensor(oh[:, k, :, :], m.eid.unsqueeze(1).to_broadcast([P, TILES, E1]),
                                           fidx[:, k, :].unsqueeze(2).to_broadcast([P, TILES, E1]), ALU.is_equal))
                then(dve.tensor_tensor(oh[:, 2, :, :], oh[:, 0, :, :], oh[:, 1, :, :], ALU.add))
                then(dve.tensor_copy(base[:, 0, :], base[:, TILES, :]))
                dve.wait_ge(s.counts, 1)
                for i in range(TILES):
                    then(dve.tensor_tensor(base[:, i + 1, :], base[:, i, :], m.bank[2][:, bass.ts(i, E1)], ALU.add))
                then(dve.tensor_tensor(pos, base[:, 0:TILES, :], m.bank[1][:, 0:TILES * E1].rearrange("p (i e) -> p i e", e=E1), ALU.add))
                for k in range(2):
                    place, keep, slot, near = (tmp[:, 4 * k + q, :] for q in range(4))
                    then(dve.tensor_tensor(oh[:, k, :, :], oh[:, k, :, :], pos, ALU.mult))
                    then(dve.tensor_reduce(place, oh[:, k, :, :], AX_X, ALU.add))
                    then(dve.tensor_scalar(keep, place, float(CAP), None, ALU.is_lt))
                    then(dve.scalar_tensor_tensor(slot, fidx[:, k, :], float(CAP), place, ALU.mult, ALU.add))
                    then(dve.scalar_tensor_tensor(slot, keep, -FAR, slot, ALU.mult, ALU.add))
                    then(dve.tensor_scalar(m.sidx[:, k, :], slot, FAR, None, ALU.add))
                    then(dve.tensor_scalar(near, place, float(CAP - 1), None, ALU.min))
                    then(dve.scalar_tensor_tensor(near, fidx[:, k, :], float(CAP), near, ALU.mult, ALU.add))
                    then(dve.tensor_copy(m.gidx[:, k, :], near))
                    ins = dve.tensor_tensor(m.diff[:, k, :], top[:, :, k], top[:, :, 1 - k], ALU.subtract)
                    then(ins)
                    ins = dve.sem_inc(s.base_ok, 1)
                    dve.wait_ge(s.gates, 2 * k + 1)
                    dve.tensor_tensor(m.gate[:, k, :], m.gate[:, k, :], keep, ALU.mult).then_inc(s.gates, 1)

            @block.scalar
            def _(act):
                for k in range(2):
                    act.wait_ge(s.base_ok, k + 1)
                    act.activation(m.gate[:, k, :], m.diff[:, k, :], ACT.Sigmoid).then_inc(s.gates, 1)

            @block.gpsimd
            def _(pool):
                pool.wait_ge(s.x_in, 48)
                for k in range(2):
                    pool.wait_ge(s.base_ok, k + 1)
                    for i in range(TILES):
                        pool.indirect_dma_start(io.xd, bass.IndirectOffsetOnAxis(ap=m.sidx[:, k, i:i + 1], axis=0), m.xn[:, i, :], None,
                                                bounds_check=SLOTS - 1, oob_is_err=False).then_inc(m.scattered, 16)
                pool.wait_ge(m.scattered, (b + 1) * (16 * 2 * TILES))
        s.clear()


def run_experts(nc, io, m):
    with ExitStack() as ctx:
        s = stage_sems(nc, ctx, "exp", "w0 w1 x0 x1 turned xt hid gelu prod out y st0 st1 wfree")
        wl, xl, st = (s.w0, s.w1), (s.x0, s.x1), (s.st0, s.st1)
        TURN, HID = [m.bank[0], m.bank[1]], [m.pair[1], m.pair[2]]
        Y = m.pair[3]
        T0, X0, H0, G0, O0, Y0, S0 = 4, 2, 8, 2, 4, 2, 16
        PER = 2 * BLOCKS

        with nc.Block() as block:

            @block.sync
            def _(sp):
                def weights(e, buf):
                    sp.dma_start(m.w1[:, buf, :, :], io.eW1[bass.ds(e, 1), :, :].rearrange("o (c p) f -> p (o c) f", p=P)).then_inc(wl[buf], 16)
                    sp.dma_start(m.w2[:, buf, :, :], io.eW2[bass.ds(e, 1), :, :].rearrange("o (c p) d -> p (o c) d", p=P)).then_inc(wl[buf], 16)

                def rows_out(n, c):
                    sp.wait_ge(s.y, 2 * n + 2 + Y0)
                    sp.dma_start(io.yd[bass.ds(n * ROWS, ROWS), :].rearrange("(i p) d -> p i d", p=P), m.yout[:, c % 2, :, :]).then_inc(st[c % 2], 16)

                weights(0, 0)
                sp.wait_ge(s.turned, T0)
                sp.dma_start(m.xin[:, 0, :, :], io.xd[0:ROWS, :].rearrange("(i p) d -> p i d", p=P)).then_inc(xl[0], 16)
                with sp.Fori(0, E1 // 2) as g:
                    for e in range(2):
                        sp.wait_ge(s.wfree, 2 * g + e + 1)
                        weights((2 * g + e + 1) % E1, 1 - e)
                        for c in range(e * BLOCKS, (e + 1) * BLOCKS):
                            n = PER * g + c
                            sp.wait_ge(s.turned, 2 * n + T0)
                            nxt = (n + 1) % (E1 * BLOCKS)
                            sp.dma_start(m.xin[:, (c + 1) % 2, :, :], io.xd[bass.ds(nxt * ROWS, ROWS), :].rearrange("(i p) d -> p i d", p=P)).then_inc(xl[(c + 1) % 2], 16)
                            rows_out(n, c)
                sp.wait_ge(st[0], 16 * E1 * BLOCKS // 2 + S0)
                sp.wait_ge(st[1], 16 * E1 * BLOCKS // 2 + S0)
                sp.wait_ge(xl[0], 16 * (E1 * BLOCKS // 2 + 1))
                sp.wait_ge(wl[0], 32 * (E1 // 2 + 1))

            @block.tensor
            def _(pe):
                pe.sem_inc(s.turned, T0)
                pe.sem_inc(s.hid, H0)
                pe.sem_inc(s.out, O0)
                pe.sem_inc(s.wfree, 1)

                def turn(n, c, loads):
                    pe.wait_ge(xl[c % 2], loads)
                    pe.wait_ge(s.xt, 2 * n - 2 + 2 + X0)
                    for k in range(KD):
                        for q in range(4):
                            t = pe.transpose(TURN[k][:, bass.ts(q, P)], m.xin[:, c % 2, q, bass.ts(k, P)], m.ident)
                        t.then_inc(s.turned, 1)

                def hidden(n, c, e, mt):
                    pe.wait_ge(s.prod, 4 * n + mt - 1 + G0)
                    for half in range(2):
                        for k in range(KD):
                            col = half * I1 + mt * P
                            mm = pe.matmul(HID[mt % 2][:, half, :], m.w1[:, e, k, col:col + P], m.xt[:, c % 2, k, :],
                                           start=(k == 0), stop=(k == KD - 1))
                    mm.then_inc(s.hid, 1)

                def outputs(n, c, e):
                    for k in range(4):
                        pe.wait_ge(s.prod, 4 * n + k + 1 + G0)
                        for r in range(4):
                            if k == 0 and r % 2 == 0:
                                pe.wait_ge(s.y, 2 * n + r // 2 - 1 + Y0)
                            mm = pe.matmul(Y[:, r // 2, (r % 2) * D:(r % 2 + 1) * D], m.ht[:, c % 2, k, bass.ts(r, P)], m.w2[:, e, k, :],
                                           start=(k == 0 and r % 2 == 0), stop=(k == 3), skip_group_check=True)
                            if k == 3 and r % 2:
                                mm.then_inc(s.out, 1)

                pe.wait_ge(xl[0], 16)
                for k in range(KD):
                    for q in range(4):
                        t = pe.transpose(TURN[k][:, bass.ts(q, P)], m.xin[:, 0, q, bass.ts(k, P)], m.ident)
                    t.then_inc(s.turned, 1)
                with pe.Fori(0, E1 // 2) as g:
                    for e in range(2):
                        pe.wait_ge(wl[e], 32 * (g + 1))
                        for c in range(e * BLOCKS, (e + 1) * BLOCKS):
                            n = PER * g + c
                            pe.wait_ge(s.xt, 2 * n + 2 + X0)
                            for mt in range(4):
                                hidden(n, c, e, mt)
                            turn(n + 1, c + 1, 16 * (BLOCKS * g + (c + 1) // 2 + 1))
                            outputs(n, c, e)
                        pe.sem_inc(s.wfree, 1)

            @block.scalar
            def _(act):
                act.sem_inc(s.xt, X0)

                def evac(n, c):
                    act.wait_ge(s.hid, 4 * n - 4 + H0)
                    for k in range(KD):
                        act.wait_ge(s.turned, 2 * n + k + 1 + T0)
                        act.copy(m.xt[:, c % 2, k, :], TURN[k]).then_inc(s.xt, 1)

                act.wait_ge(s.hid, H0)
                for k in range(KD):
                    act.wait_ge(s.turned, k + 1 + T0)
                    act.copy(m.xt[:, 0, k, :], TURN[k]).then_inc(s.xt, 1)
                with act.Fori(0, E1 // 2) as g:
                    for c in range(PER):
                        n = PER * g + c
                        for mt in range(4):
                            act.wait_ge(s.hid, 4 * n + mt + 1 + H0)
                            act.wait_ge(s.prod, 4 * n + mt - 1 + G0)
                            act.activation(m.g[:, mt % 2, :], HID[mt % 2][:, 0, :], ACT.Gelu).then_inc(s.gelu, 1)
                        evac(n + 1, c + 1)

            @block.vector
            def _(dve):
                dve.sem_inc(s.prod, G0)
                dve.sem_inc(s.y, Y0)
                dve.sem_inc(st[0], S0)
                dve.sem_inc(st[1], S0)
                with dve.Fori(0, E1 // 2) as g:
                    for c in range(PER):
                        n = PER * g + c
                        dve.wait_ge(s.out, 2 * n - 2 + O0)
                        for mt in range(4):
                            dve.wait_ge(s.gelu, 4 * n + mt + 1)
                            dve.tensor_tensor(m.ht[:, c % 2, mt, :], m.g[:, mt % 2, :], HID[mt % 2][:, 1, :], ALU.mult).then_inc(s.prod, 1)
                        dve.wait_ge(st[c % 2], 16 * (BLOCKS * g + c // 2) + S0)
                        for j in range(2):
                            dve.wait_ge(s.out, 2 * n + j + 1 + O0)
                            dve.tensor_copy(m.yout[:, c % 2, 2 * j:2 * j + 2, :].rearrange("p i d -> p (i d)"), Y[:, j, :]).then_inc(s.y, 1)
        s.clear()


def build_second_ffn(nc, io):
    with ExitStack() as ctx:
        t = {}

        def sb(name, shape, dt=F32, c=ctx):
            t[name] = c.enter_context(nc.sbuf_tensor("ff_" + name, shape, dt))[:]
        ps = ctx.enter_context(nc.psum_tensor("ff_ps", [P, 8, BANK], F32))
        t["bank"] = [ps[:, i, :] for i in range(8)]
        t["pair"] = [ps[:, 2 * i:2 * i + 2, :] for i in range(4)]
        sb("ident", [P, P])
        sb("gidx", [P, 2, TILES], U32); sb("gate", [P, 2, TILES])
        m = named(**t)
        with ExitStack() as c2:
            sb("xT", [P, KD, L], F32, c2); sb("xn", [P, TILES, D], F32, c2)
            sb("wg", [P, KD, E1], F32, c2); sb("before", [P, P], F32, c2); sb("ones", [P, P], F32, c2)
            sb("eid", [P, E1], F32, c2); sb("zero", [P, 16 * D], F32, c2)
            sb("lg", [P, TILES, E1], F32, c2); sb("top", [P, TILES, 8], F32, c2); sb("idx", [P, TILES, 8], U32, c2)
            sb("fidx", [P, 2, TILES], F32, c2); sb("oh", [P, 3, TILES, E1], F32, c2); sb("pos", [P, TILES, E1], F32, c2)
            sb("base", [P, TILES + 1, E1], F32, c2); sb("tmp", [P, 8, TILES], F32, c2); sb("sidx", [P, 2, TILES], U32, c2)
            sb("diff", [P, 2, TILES], F32, c2)
            m = named(**t)
            s = stage_sems(nc, c2, "ff_load", "w_in zero zeroed")
            with nc.Block() as block:

                @block.sync
                def _(sp):
                    for t, v in ((m.ident, io.ident), (m.wg, io.WgT.rearrange("(c p) n -> p c n", p=P)), (m.before, io.before),
                                 (m.eid, io.eid)):
                        sp.dma_start(t, v).then_inc(s.w_in, 16)
                    sp.wait_ge(s.zero, 1)
                    zd = io.xd.rearrange("(n p q) d -> n p (q d)", p=P, q=16)
                    for n in range(SLOTS // (P * 16)):
                        sp.dma_start(zd[n], m.zero).then_inc(s.zeroed, 16)
                    sp.wait_ge(s.zeroed, 16 * (SLOTS // (P * 16)))
                    sp.wait_ge(s.w_in, 64)

                @block.vector
                def _(dve):
                    dve.memset(m.zero, 0.0).then_inc(s.zero, 1)
                    dve.memset(m.ones, 1.0)
                    dve.memset(m.base, 0.0)
            s.clear()
            t["scattered"] = c2.enter_context(nc.semaphore("scattered"))
            m = named(**t)
            with nc.Fori(0, B) as b:
                route_batch(nc, b, io, m)
        with ExitStack() as c2:
            sb("w1", [P, 2, KD, 2 * I1], F32, c2); sb("w2", [P, 2, 4, D], F32, c2)
            sb("xin", [P, 2, 4, D], F32, c2); sb("xt", [P, 2, KD, ROWS], F32, c2)
            sb("g", [P, 2, ROWS], F32, c2); sb("ht", [P, 2, 4, ROWS], F32, c2); sb("yout", [P, 2, 4, D], F32, c2)
            m = named(**t)
            run_experts(nc, io, m)




H1, HD = 16, 16
SCALE = HD ** -0.5
LAMBDA_INIT = 0.8
HEADS = B * H1
STACK = 6 * HD
QB = 1024
KT = L // P
FT = 4
PARTS_Q, PARTS_K = ((0, 3), (0, 2), (0, 1)), ((0, 3), (1, 2), (2, 1))


def project_batch(nc, b, io, m):
    with ExitStack() as ctx:
        s = stage_sems(nc, ctx, "project", "x_in proj out p1 r1 p2 p3 v v_out stored")
        full, p1, p2, p3, r1 = m.full, m.p1, m.p2, m.p3, m.r1
        with nc.Block() as block:

            @block.sync
            def _(sp):
                for k in range(KD):
                    sp.dma_start(m.xT[:, k, :], io.xnT[bass.ts(b, 1), k, :, :].rearrange("o p t -> p (o t)")).then_inc(s.x_in, 16)
                for w, dst in enumerate((io.qp, io.kp)):
                    for part, t, done in ((0, p1, s.p1), (1, p2, s.p2), (2, p3, s.p3)):
                        sp.wait_ge(done, w + 1)
                        for k in range(KD):
                            v = dst[bass.ts(b, 1), 8 * k:8 * k + 8, part, :, :].rearrange("o h d t -> (o h) d t")
                            sp.dma_start(v, t[:, k, :]).then_inc(s.stored, 16)
                sp.wait_ge(s.v_out, TILES)
                sp.dma_start(io.vp[bass.ts(b, 1), :, :, :].rearrange("o h p t -> p (o h) t"),
                             m.v.rearrange("p h i c -> p h (i c)")).then_inc(s.stored, 16)
                sp.wait_ge(s.stored, 16 * 13)

            @block.tensor
            def _(pe):
                pe.wait_ge(s.x_in, 32)
                for w, wt in enumerate((m.wq, m.wk)):
                    for j in range(8):
                        k, g = j // 4, j % 4
                        if w:
                            pe.wait_ge(s.out, j + 1)
                        for c in range(KD):
                            mm = pe.matmul(m.bank[j], wt[:, c, bass.ts(k, P)], m.xT[:, c, bass.ts(g, BANK)],
                                           start=(c == 0), stop=(c == KD - 1))
                        mm.then_inc(s.proj, 1)
                pe.wait_ge(s.out, 16)
                for i in range(TILES):
                    if i >= 8:
                        pe.wait_ge(s.v_out, i - 7)
                    for c in range(KD):
                        mm = pe.matmul(m.bank[i % 8][:, 0:D], m.xT[:, c, bass.ts(i, P)], m.wv[:, c, :],
                                       start=(c == 0), stop=(c == KD - 1))
                    mm.then_inc(s.v, 1)

            @block.scalar
            def _(act):
                for w, bias in enumerate((m.bq, m.bk)):
                    for j in range(8):
                        k, g = j // 4, j % 4
                        act.wait_ge(s.proj, 8 * w + j + 1)
                        if w:
                            act.wait_ge(s.r1, 1)
                        act.activation(full[:, k, bass.ts(g, BANK)], m.bank[j], ACT.Identity, bias=bias[:, k:k + 1]).then_inc(s.out, 1)
                    act.wait_ge(s.out, 8 * w + 8)
                    if w:
                        act.wait_ge(s.stored, 16 * 6)
                    act.copy(p1, full).then_inc(s.p1, 1)
                    act.wait_ge(s.r1, w + 1)
                    act.copy(p2, r1).then_inc(s.p2, 1)

            @block.vector
            def _(dve):
                for w in range(2):
                    dve.wait_ge(s.p1, w + 1)
                    if w:
                        dve.wait_ge(s.p3, w)
                    dve.tensor_tensor(r1, full, p1, ALU.subtract).then_inc(s.r1, 1)
                    dve.wait_ge(s.p2, w + 1)
                    dve.wait_ge(s.r1, w + 1)
                    dve.tensor_tensor(p3, r1, p2, ALU.subtract).then_inc(s.p3, 1)
                for i in range(TILES):
                    dve.wait_ge(s.v, i + 1)
                    dve.tensor_tensor(m.v[:, :, i, 0:HD], m.bank[i % 8][:, 0:D].rearrange("p (h d) -> p h d", d=HD),
                                      m.bv.rearrange("p (h d) -> p h d", d=HD), ALU.add).then_inc(s.v_out, 1)
        s.clear()


def combine_experts(pool, io, m):
    PARTS = TILES // FT
    MOVED = 16 * (2 * FT + 1)
    pool.memset(m.units, 1.0).then_inc(m.gate_ready, 1)
    pool.wait_ge(m.gate_ready, 1)
    with pool.Fori(0, B) as b:
        pool.dma_start(m.gidx, io.places[bass.ts(b, 1), :, :, :].rearrange("o p k i -> (o p) k i")).then_inc(m.looked_up, 16)
        pool.dma_start(m.gate_in, io.gates[bass.ts(b, 1), :, :, :].rearrange("o p k i -> (o p) k i")).then_inc(m.looked_up, 16)
        pool.wait_ge(m.looked_up, 32 * (b + 1))
        pool.tensor_tensor(m.gate, m.gate_in, m.units, ALU.mult).then_inc(m.gate_ready, 1)
        for part in range(PARTS):
            done = PARTS * b + part
            for i in range(FT):
                for k in range(2):
                    place = m.gidx[:, k, FT * part + i:FT * part + i + 1]
                    pool.indirect_dma_start(m.y[:, k, i, :], None, io.yd, bass.IndirectOffsetOnAxis(ap=place, axis=0),
                                            bounds_check=SLOTS - 1, oob_is_err=False).then_inc(m.moved, 16)
            pool.wait_ge(m.gate_ready, b + 2)
            pool.wait_ge(m.moved, MOVED * done + 32 * FT)
            gates = m.gate[:, :, bass.ts(part, FT)].unsqueeze(3).to_broadcast([P, 2, FT, D])
            pool.tensor_tensor(m.y, m.y, gates, ALU.mult).then_inc(m.gated, 1)
            pool.wait_ge(m.gated, done + 1)
            pool.tensor_tensor(m.fsum, m.y[:, 0, :, :], m.y[:, 1, :, :], ALU.add).then_inc(m.summed, 1)
            pool.wait_ge(m.summed, done + 1)
            pool.dma_start(io.f[bass.ts(b, 1), :, part, :].rearrange("o p n -> (o p) n"),
                           m.fsum.rearrange("p i d -> p (i d)")).then_inc(m.moved, 16)
    pool.wait_ge(m.moved, MOVED * PARTS * B)


def attend(nc, io, m):
    with ExitStack() as ctx:
        s = stage_sems(nc, ctx, "att", "init loaded v_loaded score ex av o_copy o2 ring ring_free mpart mfin mneg mhi mlo mrow rec a_out")
        S, O, ring = [m.pair[0], m.pair[1]], m.pair[2], [m.bank[6], m.bank[7]]
        NRING = 34
        PRO = 65
        EX0, AV0, RF0 = 2, 4, 2
        ROUND, QUARTER, LAG = 4, 256, 6

        with nc.Block() as block:

            @block.sync
            def _(sp):
                def load(h, buf):
                    src_q, src_k = io.qp.rearrange("b h n d t -> (b h) n d t"), io.kp.rearrange("b h n d t -> (b h) n d t")
                    row = 0
                    for (q0, nq), (k0, nk) in zip(PARTS_Q, PARTS_K):
                        sp.dma_start(m.qs[row:row + HD * nq, buf, :],
                                     src_q[bass.ds(h, 1), q0:q0 + nq, :, :].rearrange("o n d t -> (o n d) t")).then_inc(s.loaded, 16)
                        for r in range(nq):
                            sp.dma_start(m.ks[row + HD * r:row + HD * (r + 1), buf, :],
                                         src_k[bass.ds(h, 1), k0, :, :].rearrange("o d t -> (o d) t")).then_inc(s.loaded, 16)
                        row += HD * nq

                def load_v(h, buf):
                    sp.dma_start(m.vst[:, buf, :, :], io.vp.rearrange("b h p t -> (b h) p t")[bass.ds(h, 1), :, :].rearrange("o p (i c) -> p (o i) c", c=32)).then_inc(s.v_loaded, 16)

                def rows(step, half, buf):
                    sp.wait_ge(s.mlo, step + 1)
                    for r in range(2):
                        sp.dma_start(m.qs[STACK + r:STACK + r + 1, buf, half * QB:(half + 1) * QB],
                                     m.mrow[:, r, :]).then_inc(s.mrow, 16)

                LOAD = 16 * 9
                sp.wait_ge(s.init, 3)
                load(0, 0)
                sp.wait_ge(s.loaded, LOAD)
                load(1, 1)
                load_v(0, 0)
                rows(0, 0, 0)
                with sp.Fori(0, HEADS // 4) as g:
                    for j in range(4):
                        h = 4 * g + j
                        sp.wait_ge(s.loaded, LOAD * (h + 2))
                        sp.wait_ge(s.score, 16 * (2 * h) + 1)
                        load((h + 2) % HEADS, (j + 2) % 4)
                        sp.wait_ge(s.v_loaded, 16 * (h + 1))
                        sp.wait_ge(s.av, 8 * (2 * h) + 3 + AV0)
                        load_v((h + 1) % HEADS, (j + 1) % 2)
                        rows(2 * h + 1, 1, j)
                        rows(2 * h + 2, 0, (j + 1) % 4)
                sp.wait_ge(s.loaded, LOAD * (HEADS + 2))
                sp.wait_ge(s.v_loaded, 16 * (HEADS + 1))
                sp.wait_ge(s.mrow, 32 * (2 * HEADS + 1))

            @block.gpsimd
            def _(pool):
                pool.memset(m.E[:, 8:16, :], 1.0).then_inc(s.init, 1)
                pool.wait_ge(s.init, 1)
                pool.memset(m.vst[:, 1, :, :], 1.0).then_inc(s.init, 1)
                pool.wait_ge(s.init, 2)
                pool.memset(m.ks[STACK:P, :, :], 1.0).then_inc(s.init, 1)
                pool.wait_ge(s.init, 3)
                combine_experts(pool, io, m)

            @block.tensor
            def _(pe):
                def peak(i, c, buf, n, wait):
                    pe.wait_ge(s.ring_free, wait)
                    pe.matmul(ring[n % 2], m.qs[0:STACK, buf, bass.ts(i, P)], m.ks[0:STACK, buf, bass.ts(c, BANK)],
                              start=True, stop=True).then_inc(s.ring, 1)

                def turn(n, wait, mf):
                    pe.wait_ge(s.mfin, mf)
                    pe.wait_ge(s.ring_free, wait)
                    pe.transpose(ring[n % 2][0:8, 0:P], m.mx[:], m.ident[:]).then_inc(s.ring, 1)

                def values(r, quarter, par):
                    cols = slice(QUARTER * (quarter % 2), QUARTER * (quarter % 2 + 1))
                    for q in range(ROUND):
                        kt = ROUND * r + q
                        mm = pe.matmul(O[32 * q:32 * q + 32, quarter // 2, cols], m.vst[:, par, kt, :], m.E[:, kt, bass.ts(quarter, QUARTER)],
                                       start=(r == 0 and quarter % 2 == 0), stop=(r == 3), skip_group_check=True)
                    if quarter % 2:
                        mm.then_inc(s.av, 1)

                def normalise(t, n, wait, t1):
                    pe.wait_ge(s.o_copy, t1)
                    pe.wait_ge(s.ring_free, wait)
                    for i in range(8):
                        mm = pe.matmul(ring[n % 2][:, 17 * i:17 * i + 17], m.osb[:, bass.ts(i, P)], m.selsum[:], start=True, stop=True)
                    mm.then_inc(s.ring, 1)

                LOAD = 16 * 9
                pe.wait_ge(s.init, 3)
                pe.wait_ge(s.loaded, LOAD)
                n = 0
                for half in range(2):
                    for i in range(8):
                        for c in range(4):
                            peak(8 * half + i, c, 0, n, n + 1)
                            n += 1
                    if half == 0:
                        turn(n, n + 1, 1)
                        n += 1
                assert n == PRO
                for q in range(ROUND):
                    for bank in range(2):
                        pe.matmul(O[32 * q:32 * q + 32, bank, :], m.vst[:, 1, q, :], m.E[:, 8 + q, bass.ts(bank, BANK)],
                                  start=True, stop=True, skip_group_check=True)

                def step(h, t, j, half):
                    local = 0
                    nxt = (j + 1) % 4

                    def w():
                        return PRO + NRING * t + local + 1
                    pe.wait_ge(s.mrow, 32 * (t + 1))
                    if half == 0:
                        pe.wait_ge(s.loaded, LOAD * (h + 2))
                        pe.wait_ge(s.v_loaded, 16 * (h + 1))
                    for kt in range(KT):
                        pe.wait_ge(s.ex, 16 * t + kt - 2 + 1 + EX0)
                        for hf in range(2):
                            mm = pe.matmul(S[kt % 2][:, hf, :], m.ks[0:STACK + 2, j, bass.ts(kt, P)],
                                           m.qs[0:STACK + 2, j, half * QB + hf * BANK:half * QB + (hf + 1) * BANK],
                                           start=True, stop=True)
                        mm.then_inc(s.score, 1)
                        peak(8 * half + kt // 2, 2 * kt % 4, nxt, PRO + local, w())
                        local += 1
                        if kt == 3:
                            turn(PRO + local, w(), t + 2)
                            local += 1
                        if kt == 9:
                            normalise(t, PRO + local, w(), 2 * t + 2)
                            local += 1
                        r, quarter = (kt - LAG) // ROUND % ROUND, (kt - LAG) % ROUND
                        if quarter == 0:
                            pe.wait_ge(s.ex, 16 * t + ROUND * ((kt - LAG) // ROUND + 1) + EX0)
                        if r == 0 and quarter % 2 == 0:
                            pe.wait_ge(s.o_copy, 2 * t + quarter // 2 + 1)
                        values(r, quarter, (j if half or kt >= LAG else j + 1) % 2)
                        peak(8 * half + kt // 2, 2 * kt % 4 + 1, nxt, PRO + local, w())
                        local += 1
                    assert local == NRING

                with pe.Fori(0, HEADS // 4) as g:
                    for j in range(4):
                        for half in range(2):
                            step(4 * g + j, 8 * g + 2 * j + half, j, half)
                t = 2 * HEADS
                pe.wait_ge(s.ex, 16 * t + EX0)
                for y in range(16 - LAG, 16):
                    values(y // ROUND, y % ROUND, (HEADS - 1) % 2)
                normalise(t, PRO, PRO + NRING * t + 1, 2 * t + 2)

            @block.scalar
            def _(act):
                act.sem_inc(s.ex, EX0)

                def copy_out(t, bank):
                    act.wait_ge(s.av, 8 * t + 2 + bank + AV0)
                    act.wait_ge(s.o2, t + 1)
                    act.copy(m.osb[:, bass.ts(bank, BANK)], O[:, bank, :]).then_inc(s.o_copy, 1)

                def step(t):
                    for kt in range(KT):
                        act.wait_ge(s.score, 16 * t + kt + 1)
                        if kt % ROUND == 0:
                            act.wait_ge(s.av, 8 * t + 2 * (kt // ROUND) - 3 + AV0)
                        act.activation(m.E[:, kt, :], S[kt % 2].rearrange("p a b -> p (a b)"), ACT.Exp, scale=SCALE).then_inc(s.ex, 1)
                        if kt in (3, 5):
                            copy_out(t, kt // 2 - 1)

                with act.Fori(0, HEADS) as h:
                    for half in range(2):
                        step(2 * h + half)
                copy_out(2 * HEADS, 0)
                copy_out(2 * HEADS, 1)

            @block.vector
            def _(dve):
                dve.sem_inc(s.ring_free, RF0)
                dve.sem_inc(s.av, AV0)
                dve.sem_inc(s.o2, 1)

                def peak(job, n, ready):
                    dve.wait_ge(s.ring, ready)
                    dve.tensor_reduce(m.mpart[:, job:job + 1], ring[n % 2], AX_X, ALU.max).then_inc(s.ring_free, 1)

                def last(t, ready):
                    dve.wait_ge(s.ring_free, ready + RF0)
                    dve.tensor_reduce(m.mx[:], m.mpart[:].rearrange("p (i c) -> p i c", c=4), AX_X, ALU.max).then_inc(s.mfin, 1)

                def turn(t, n, ready, rows_out):
                    dve.wait_ge(s.ring, ready)
                    if rows_out is not None:
                        dve.wait_ge(s.mrow, rows_out)
                    dve.tensor_scalar(m.mneg[:], ring[n % 2][0:8, 0:P], -1.0, None, ALU.mult).then_inc(s.ring_free, 1)
                    dve.wait_ge(s.ring_free, ready + RF0)
                    dve.tensor_copy(m.mrow[:, 0, :], m.mneg[:]).then_inc(s.mhi, 1)
                    dve.wait_ge(s.mhi, t + 1)
                    dve.tensor_tensor(m.mrow[:, 1, :], m.mneg[:], m.mrow[:, 0, :], ALU.subtract).then_inc(s.mlo, 1)

                def normalise(slot, half, t, n, ready):
                    dve.wait_ge(s.ring, ready)
                    o = ring[n % 2][:, 0:8 * 17].rearrange("p (i c) -> p i c", c=17)
                    dve.sem_inc(s.o2, 1)
                    dve.wait_ge(s.a_out, t + 1)
                    dve.reciprocal(m.rec[:], o[:, :, 16:17]).then_inc(s.rec, 1)
                    dve.wait_ge(s.rec, t + 1)
                    dve.tensor_tensor(m.A[:, bass.ds(slot, 1), 8 * half:8 * half + 8, :].rearrange("p o i d -> p (o i) d"),
                                      o[:, :, 0:HD], m.rec[:].to_broadcast([P, 8, HD]), ALU.mult).then_inc(s.a_out, 1)
                    dve.wait_ge(s.a_out, t + 2)
                    dve.sem_inc(s.ring_free, 1)

                dve.sem_inc(s.a_out, 1)
                n = 0
                for half in range(2):
                    if half:
                        dve.wait_ge(s.mfin, 1)
                    for i in range(32):
                        peak(i, n, n + 1)
                        n += 1
                    last(half, n)
                    if half == 0:
                        turn(0, n, n + 1, None)
                        n += 1

                def step(h, t, half):
                    local = 0
                    dve.wait_ge(s.mfin, t + 2)
                    for job in range(32):
                        peak(job, PRO + local, PRO + NRING * t + local + 1)
                        local += 1
                        if job == 6:
                            turn(t + 1, PRO + local, PRO + NRING * t + local + 1, 32 * (t + 1))
                            local += 1
                        if job == 18:
                            normalise(h + half, 1 - half, t, PRO + local, PRO + NRING * t + local + 1)
                            local += 1
                    last(t, PRO + NRING * t + local)

                with dve.Fori(0, HEADS) as h:
                    for half in range(2):
                        step(h, 2 * h + half, half)
                t = 2 * HEADS
                normalise(HEADS, 1, t, PRO, PRO + NRING * t + 1)
        s.clear()


def output_batch(nc, b, io, m):
    with ExitStack() as ctx:
        s = stage_sems(nc, ctx, "output", "f_in x_in mix turned evac out s_out sig silu prod sum stored")
        PARTS = TILES // FT
        with nc.Block() as block:

            @block.vector
            def _(dve):
                for g in range(PARTS):
                    for k in range(KD):
                        src = m.A[:, bass.ds(b * H1 + 1 + 8 * k, 8), :, :]
                        for i in range(FT * g, FT * (g + 1)):
                            dst = m.mix[:, i, bass.ts(k, P)].rearrange("p (h d) -> p h d", d=HD)
                            if k == 0:
                                x2 = m.A[:, bass.ds(b * H1 + 9, 8), :, :]
                                dve.scalar_tensor_tensor(dst, x2[:, :, i, :], m.nlam[:, 0:1], src[:, :, i, :],
                                                         ALU.mult, ALU.add).then_inc(s.mix, 1)
                            else:
                                dve.tensor_copy(dst, src[:, :, i, :]).then_inc(s.mix, 1)
                for g in range(PARTS):
                    tiles = bass.ts(g, FT)
                    for i in range(FT * g, FT * (g + 1)):
                        dve.wait_ge(s.out, i + 1)
                        dve.tensor_tensor(m.s[:, i, :], m.bank[i % 8][:, 0:D], m.bp[:], ALU.add).then_inc(s.s_out, 1)
                    dve.wait_ge(s.silu, g + 1)
                    dve.wait_ge(s.s_out, FT * (g + 1))
                    dve.tensor_tensor(m.s[:, tiles, :], m.s[:, tiles, :], m.f[:, tiles, :], ALU.mult).then_inc(s.prod, 1)

            @block.gpsimd
            def _(pool):
                for g in range(PARTS):
                    tiles = bass.ts(g, FT)
                    pool.wait_ge(s.sig, g + 1)
                    pool.tensor_tensor(m.f[:, tiles, :], m.f[:, tiles, :], m.sig[:, tiles, :], ALU.mult).then_inc(s.silu, 1)
                for g in range(PARTS):
                    tiles = bass.ts(g, FT)
                    pool.wait_ge(s.x_in, 16)
                    pool.wait_ge(s.prod, g + 1)
                    pool.tensor_tensor(m.x1[:, tiles, :], m.x1[:, tiles, :], m.s[:, tiles, :], ALU.add).then_inc(s.sum, 1)

            @block.tensor
            def _(pe):
                for g in range(4):
                    pe.wait_ge(s.mix, 2 * FT * (g + 1))
                    for k in range(KD):
                        for q in range(4):
                            t = pe.transpose(m.bank[g * KD + k][:, bass.ts(q, P)], m.mix[:, 4 * g + q, bass.ts(k, P)], m.ident[:])
                        t.then_inc(s.turned, 1)
                pe.wait_ge(s.evac, 8)
                for i in range(TILES):
                    if i >= 8:
                        pe.wait_ge(s.s_out, i - 7)
                    for c in range(KD):
                        mm = pe.matmul(m.bank[i % 8][:, 0:D], m.outT[:, c, bass.ts(i, P)], m.wp[:, c, :],
                                       start=(c == 0), stop=(c == KD - 1))
                    mm.then_inc(s.out, 1)

            @block.scalar
            def _(act):
                act.wait_ge(s.f_in, 16)
                for g in range(PARTS):
                    tiles = bass.ts(g, FT)
                    act.activation(m.sig[:, tiles, :], m.f[:, tiles, :], ACT.Sigmoid).then_inc(s.sig, 1)
                for g in range(4):
                    for k in range(KD):
                        act.wait_ge(s.turned, g * KD + k + 1)
                        act.copy(m.outT[:, k, bass.ts(g, BANK)], m.bank[g * KD + k]).then_inc(s.evac, 1)

            @block.sync
            def _(sp):
                sp.dma_start(m.f, io.f[bass.ts(b, 1), :, :, :].rearrange("o p g (i d) -> (o p) (g i) d", d=D)).then_inc(s.f_in, 16)
                sp.dma_start(m.x1, io.x1[bass.ts(b, 1), :, :].rearrange("o (i p) d -> p (o i) d", p=P)).then_inc(s.x_in, 16)
                out = io.out[bass.ts(b, 1), :, :].rearrange("o (i p) d -> p (o i) d", p=P)
                for g in range(PARTS):
                    sp.wait_ge(s.sum, g + 1)
                    sp.dma_start(out[:, bass.ts(g, FT), :], m.x1[:, bass.ts(g, FT), :]).then_inc(s.stored, 16)
                sp.wait_ge(s.stored, 16 * PARTS)
        s.clear()


def build_attention(nc, io):
    with ExitStack() as ctx:
        t = {}

        def sb(name, shape, dt=F32, c=ctx):
            t[name] = c.enter_context(nc.sbuf_tensor("at_" + name, shape, dt))[:]
        ps = ctx.enter_context(nc.psum_tensor("at_ps", [P, 8, BANK], F32))
        t["bank"] = [ps[:, i, :] for i in range(8)]
        t["pair"] = [ps[:, 2 * i:2 * i + 2, :] for i in range(4)]
        sb("ident", [P, P])
        sb("wp", [P, KD, D]); sb("bp", [P, D])
        sb("nlam", [P, 1])
        m = named(**t)
        with ExitStack() as c2:
            for n in ("wq", "wk", "wv"):
                sb(n, [P, KD, D], F32, c2)
            sb("bq", [P, KD], F32, c2); sb("bk", [P, KD], F32, c2); sb("bv", [P, D], F32, c2)
            sb("xT", [P, KD, L], F32, c2); sb("full", [P, KD, L], F32, c2); sb("r1", [P, KD, L], F32, c2)
            for n in ("p1", "p2", "p3"):
                sb(n, [P, KD, L], BF16, c2)
            sb("v", [P, H1, TILES, 32], F32, c2)
            sb("lam", [P, 4, P], F32, c2); sb("lsum", [P, 6, 8], F32, c2); sb("lm", [P, 2], F32, c2)
            m = named(**t)
            s = stage_sems(nc, c2, "at_load", "w_in prod sum low ex diff mean")
            with nc.Block() as block:

                @block.sync
                def _(sp):
                    loads = [(m.ident, io.ident), (m.wq, io.WqT.rearrange("(c p) n -> p c n", p=P)), (m.wk, io.WkT.rearrange("(c p) n -> p c n", p=P)),
                             (m.wv, io.WvT.rearrange("(c p) n -> p c n", p=P)), (m.wp, io.WpT.rearrange("(c p) n -> p c n", p=P)),
                             (m.bv, io.bv.partition_broadcast(P)), (m.bp, io.bp.partition_broadcast(P))]
                    for n, v in enumerate((io.lambda_q1, io.lambda_k1, io.lambda_q2, io.lambda_k2)):
                        loads.append((m.lam[:, n, :], v.rearrange("a b c -> (a b c)").partition_broadcast(P)))
                    with nc.allow_non_contiguous_dma(reason="columns of 128 numbers"):
                        for t, v in ((m.bq, io.bq), (m.bk, io.bk)):
                            sp.dma_start(t, v.rearrange("(c p) -> p c", p=P)).then_inc(s.w_in, 16)
                        for t, v in loads:
                            sp.dma_start(t, v).then_inc(s.w_in, 16)
                    sp.wait_ge(s.w_in, 16 * 13)

                @block.vector
                def _(dve):
                    dve.memset(m.v, 0.0).then_inc(s.prod, 1)
                    dve.wait_ge(s.prod, 1)
                    dve.memset(m.v[:, :, :, HD:HD + 1], 1.0).then_inc(s.prod, 1)
                    dve.wait_ge(s.w_in, 16 * 13)
                    for n in range(2):
                        dve.tensor_tensor(m.lam[:, 2 * n, :], m.lam[:, 2 * n, :], m.lam[:, 2 * n + 1, :], ALU.mult).then_inc(s.prod, 1)
                    dve.wait_ge(s.prod, 4)
                    for n in range(2):
                        dve.tensor_reduce(m.lsum[:, n, :], m.lam[:, 2 * n, :].rearrange("p (h d) -> p h d", d=HD), AX_X, ALU.add).then_inc(s.sum, 1)
                    dve.wait_ge(s.sum, 2)
                    dve.tensor_scalar(m.lsum[:, 2:4, :], m.lsum[:, 0:2, :], 5.0, None, ALU.min).then_inc(s.low, 1)
                    dve.wait_ge(s.ex, 1)
                    dve.tensor_tensor(m.lsum[:, 0, :], m.lsum[:, 4, :], m.lsum[:, 5, :], ALU.subtract).then_inc(s.diff, 1)
                    dve.wait_ge(s.diff, 1)
                    dve.tensor_scalar(m.lsum[:, 1, :], m.lsum[:, 0, :], LAMBDA_INIT, None, ALU.add).then_inc(s.diff, 1)
                    dve.wait_ge(s.diff, 2)
                    dve.tensor_reduce(m.lm[:, 0:1], m.lsum[:, 1, :], AX_X, ALU.add).then_inc(s.mean, 1)
                    dve.wait_ge(s.mean, 1)
                    dve.tensor_scalar(m.nlam, m.lm[:, 0:1], -1.0 / 8, None, ALU.mult).then_inc(s.mean, 1)

                @block.scalar
                def _(act):
                    act.wait_ge(s.low, 1)
                    act.activation(m.lsum[:, 4:6, :], m.lsum[:, 2:4, :], ACT.Exp).then_inc(s.ex, 1)
            s.clear()
            with nc.Fori(0, B) as b:
                project_batch(nc, b, io, m)
        sb("A", [P, HEADS + 1, TILES, HD])
        m = named(**t)
        with ExitStack() as c2:
            sb("E", [P, KT, QB], F32, c2)
            sb("qs", [P, 4, L], BF16, c2)
            sb("ks", [P, 4, L], BF16, c2)
            sb("vst", [P, 2, KT, 32], F32, c2)
            sb("osb", [P, QB], F32, c2)
            sb("selsum", [P, 17], F32, c2)
            sb("mpart", [P, 32], F32, c2); sb("mx", [P, 8], F32, c2); sb("mneg", [8, P], F32, c2)
            sb("mrow", [8, 2, P], BF16, c2); sb("rec", [P, 8, 1], F32, c2)
            sb("y", [P, 2, FT, D], F32, c2); sb("fsum", [P, FT, D], F32, c2); sb("gidx", [P, 2, TILES], U32, c2); sb("gate", [P, 2, TILES], F32, c2)
            sb("gate_in", [P, 2, TILES], F32, c2); sb("units", [P, 2, TILES], F32, c2)
            for n in ("looked_up", "gate_ready", "moved", "gated", "summed"):
                t[n] = c2.enter_context(nc.semaphore(n))
            m = named(**t)
            s = stage_sems(nc, c2, "at_sel", "sel_in")
            with nc.Block() as block:

                @block.sync
                def _(sp):
                    sp.dma_start(m.selsum, io.selsum).then_inc(s.sel_in, 16)
                    sp.wait_ge(s.sel_in, 16)
            s.clear()
            attend(nc, io, m)
        with ExitStack() as c2:
            sb("outT", [P, KD, L], F32, c2)
            sb("mix", [P, TILES, D], F32, c2)
            for n in ("s", "f", "sig", "x1"):
                sb(n, [P, TILES, D], F32, c2)
            m = named(**t)
            with nc.Fori(0, B) as b:
                output_batch(nc, b, io, m)



def build(nc, io):
    build_first_layer(nc, io)
    build_second_ffn(nc, io)
    build_attention(nc, io)


def kernel(**inputs):
    import numpy as np
    import concourse.bacc as bacc
    from concourse.bass_utils import run_bass_kernel_spmd as run

    nc = bacc.Bacc("TRN2", target_bir_lowering=False, num_devices=1)
    arrays, drams = {}, {}

    def put(name, x):
        x = np.ascontiguousarray(x)
        arrays[f"in_{name}"] = x
        drams[name] = nc.dram_tensor(f"in_{name}", x.shape, mybir.dt.from_np(x.dtype), kind="ExternalInput").ap()

    def scratch(name, shape, dt):
        drams[name] = nc.dram_tensor(name, shape, dt, kind="Internal").ap()

    for name, x in inputs.items():
        layer, part, short = name.split("_", 2)
        if layer == "L0":
            put(short, x)
        elif part == "attn" and short[0] == "W":
            put(short + "T", np.asarray(x).T)
        elif part == "attn":
            put(short, x)
        elif short == "Wg":
            put("WgT", np.asarray(x).T)
        else:
            put("e" + short, x)
    put("ident", np.eye(P, dtype=np.float32))
    sel = np.zeros((3, 2 * NS, 2 * NS, P), np.float32)
    for n in range(2 * NS):
        sel[:, n, n, :] = 1
    put("sel", sel.reshape(96, -1).astype(np.dtype("bfloat16")))
    selsum = np.zeros((4, 32, 17), np.float32)
    for c in range(17):
        selsum[:, c, c] = 1
    put("selsum", selsum.reshape(P, 17))
    put("before", np.triu(np.ones((P, P), np.float32), 1))
    put("eid", np.tile(np.arange(E1, dtype=np.float32), (P, 1)))

    scratch("x1", (B, L, D), F32)
    scratch("xn", (B, L, D), F32)
    scratch("xnT", (B, KD, P, L), F32)
    scratch("qp", (B, H1, 3, HD, L), BF16)
    scratch("kp", (B, H1, 3, HD, L), BF16)
    scratch("vp", (B, H1, P, TILES * 32), F32)
    scratch("f", (B, P, TILES // FT, FT * D), F32)
    scratch("xd", (SLOTS, D), F32)
    scratch("yd", (SLOTS, D), F32)
    scratch("places", (B, P, 2, TILES), U32)
    scratch("gates", (B, P, 2, TILES), F32)
    drams["out"] = nc.dram_tensor("out_0", (B, L, D), F32, kind="ExternalOutput").ap()
    build(nc, named(**drams))
    r = run(nc, [arrays], core_ids=[0])
    return r.results[0]["out_0"]
```

```python
import numpy as np
import concourse.bass as bass
from concourse import mybir
from contextlib import ExitStack
from collections import namedtuple

F32 = mybir.dt.float32
BF16 = mybir.dt.bfloat16
I32 = mybir.dt.int32
U32 = mybir.dt.uint32
ALU = mybir.AluOpType
ACT = mybir.ActivationFunctionType
AX_X = mybir.AxisListType.X

P = 128
B, L, D = 4, 2048, 256
NS = 16
T = B * L
KD = D // P
TILES = L // P
HALF = L // 2
BANK = 512
DT_MIN, DT_MAX, RMS_EPS, LN_EPS = 0.0001, 10.0, 1e-06, 1e-05
CENTER, HALFSPAN = (DT_MAX + DT_MIN) / 2.0, (DT_MAX - DT_MIN) / 2.0
LN2 = 0.6931471805599453
E0, F0 = 8, 128


def named(**parts):
    return namedtuple("Parts", parts)(**parts)


def stage_sems(nc, ctx, stage, names):
    found = {n: ctx.enter_context(nc.semaphore(f"{stage}_{n}")) for n in names.split()}

    def clear():
        nums = sorted(x.num for x in found.values())
        first = nums[0]
        for n, after in zip(nums, nums[1:] + [None]):
            if after != n + 1:
                nc.sync.sem_clear(range(first, n + 1))
                first = after
        nc.all_engine_barrier()

    return named(clear=clear, **found)


def prepare_batch(nc, b, io, m):
    with ExitStack() as ctx:
        s = stage_sems(nc, ctx, "prepare_batch", "x_in0 x_in1 x_in2 x_in3 zeroed stats mv root rstd ms root2 rr x0 xr turned evac_a evac_d z zb t_abs t_exp t_ln sp th delta lnd sq u bc bcx p1 r1 p2 r2")
        x0, xr = m.nat, m.work[:, 0:4096].rearrange("p (i d) -> p i d", i=TILES)
        t1 = m.work[:, 4096:8192].rearrange("p (k t) -> p k t", k=KD)
        bcx, r1 = m.work[0:96, 8192:10240], m.work[0:96, 10240:12288]
        p2 = m.work[0:96, 12288:13312].bitcast(BF16)
        stats, mv, sm = m.stats, m.mv, m.small
        x_in = (s.x_in0, s.x_in1, s.x_in2, s.x_in3)
        with nc.Block() as block:

            @block.sync
            def _(sp):
                for g in range(4):
                    sp.dma_start(m.x[:, bass.ts(g, 4), :], io.x[bass.ts(b, 1), bass.ts(g, BANK), :].rearrange("o (i p) d -> p (o i) d", p=P)).then_inc(x_in[g], 16)
                sp.wait_ge(s.x_in3, 16)
                sp.dma_start(io.xd[bass.ts(b, SLOTS // B), :].rearrange("(p q) d -> p q d", p=P),
                             m.zero.unsqueeze(1).to_broadcast([P, SLOTS // B // P, D])).then_inc(s.zeroed, 16)
                sp.wait_ge(s.zeroed, 16)

            @block.vector
            def _(dve):
                for i in range(TILES):
                    dve.wait_ge(x_in[i // 4], 16)
                    dve.bn_stats(stats[:, i, :], m.x[:, i, :]).then_inc(s.stats, 1)
                for i in range(TILES):
                    dve.wait_ge(s.stats, i + 1)
                    dve.bn_aggr(mv[:, i, :], stats[:, i, :]).then_inc(s.mv, 1)
                dve.wait_ge(s.root, 1)
                dve.reciprocal(sm[:, 1, :], sm[:, 0, :]).then_inc(s.rstd, 1)
                dve.wait_ge(s.rstd, 1)
                dve.tensor_tensor(sm[:, 2, :], sm[:, 1, :], sm[:, 1, :], ALU.mult).then_inc(s.ms, 1)
                dve.wait_ge(s.ms, 1)
                dve.wait_ge(s.mv, TILES)
                dve.tensor_tensor(sm[:, 3, :], sm[:, 2, :], mv[:, :, 1], ALU.mult).then_inc(s.ms, 1)
                for i in range(TILES + 2):
                    if i < TILES:
                        dve.tensor_scalar(x0[:, i, :], m.x[:, i, :], mv[:, i, 0:1], sm[:, 1, i:i + 1],
                                          ALU.subtract, ALU.mult).then_inc(s.x0, 1)
                    if i == 1:
                        dve.wait_ge(s.root2, 1)
                        dve.reciprocal(sm[:, 5, :], sm[:, 4, :]).then_inc(s.rr, 1)
                    if i >= 2:
                        dve.wait_ge(s.rr, 1)
                        dve.wait_ge(s.x0, i - 1)
                        dve.tensor_scalar(xr[:, i - 2, :], x0[:, i - 2, :], sm[:, 5, i - 2:i - 1], None, ALU.mult).then_inc(s.xr, 1)
                for g in range(4):
                    for k in range(KD):
                        dve.wait_ge(s.turned, g * KD + k + 1)
                        dve.tensor_scalar(m.xrT[:, k, bass.ts(g, BANK)], m.bank[g * KD + k][:, :], m.nw[:, k:k + 1],
                                          None, ALU.mult).then_inc(s.evac_d, 1)
                for k in range(KD):
                    dve.wait_ge(s.zb, 4 * (k + 1))
                    dve.scalar_tensor_tensor(t1[:, k, :], m.lnd[:, k, :], -1.0, m.lnd[:, k, :], ALU.mult, ALU.max).then_inc(s.t_abs, 1)
                for k in range(KD):
                    dve.wait_ge(s.t_ln, k + 1)
                    dve.scalar_tensor_tensor(m.lnd[:, k, :], m.lnd[:, k, :], 0.0, t1[:, k, :], ALU.max, ALU.add).then_inc(s.sp, 1)
                dve.wait_ge(s.p1, 1)
                dve.tensor_tensor(r1, bcx, m.bc3[:], ALU.subtract).then_inc(s.r1, 1)
                for k in range(KD):
                    dve.wait_ge(s.th, k + 1)
                    dve.tensor_scalar(m.lnd[:, k, :], m.lnd[:, k, :], HALFSPAN, CENTER, ALU.mult, ALU.add).then_inc(s.delta, 1)
                dve.wait_ge(s.p2, 1)
                dve.tensor_tensor(bcx, r1, p2, ALU.subtract).then_inc(s.r2, 1)
                dve.wait_ge(s.r1, 1)
                dve.tensor_copy(m.bc3[32:64, :], r1[32:64, :]).then_inc(s.r2, 1)
                dve.wait_ge(s.r2, 2)
                dve.tensor_copy(m.bc3[64:96, :], bcx[64:96, :]).then_inc(s.r2, 1)
                for k in range(KD):
                    dve.wait_ge(s.sq, k + 1)
                    dve.tensor_tensor(m.u[:, k, :], t1[:, k, :], m.xrT[:, k, :], ALU.mult).then_inc(s.u, 1)

            @block.scalar
            def _(act):
                act.wait_ge(s.mv, TILES)
                act.activation(sm[:, 0, :], mv[:, :, 1], ACT.Sqrt, bias=m.eps[:, 0:1]).then_inc(s.root, 1)
                act.wait_ge(s.ms, 2)
                act.activation(sm[:, 4, :], sm[:, 3, :], ACT.Sqrt, bias=m.eps[:, 1:2]).then_inc(s.root2, 1)
                for j in range(8):
                    k, g = j // 4, j % 4
                    act.wait_ge(s.z, j + 1)
                    act.activation(m.lnd[:, k, bass.ts(g, BANK)], m.bank[j][:, :], ACT.Identity,
                                   bias=m.bd[:, k:k + 1]).then_inc(s.zb, 1)
                    if j == 5:
                        act.wait_ge(s.t_abs, 1)
                        act.activation(t1[:, 0, :], t1[:, 0, :], ACT.Exp, scale=-1.0).then_inc(s.t_exp, 1)
                act.wait_ge(s.t_exp, 1)
                act.activation(t1[:, 0, :], t1[:, 0, :], ACT.Ln, bias=1.0).then_inc(s.t_ln, 1)
                act.wait_ge(s.t_abs, 2)
                act.activation(t1[:, 1, :], t1[:, 1, :], ACT.Exp, scale=-1.0).then_inc(s.t_exp, 1)
                act.wait_ge(s.t_exp, 2)
                act.activation(t1[:, 1, :], t1[:, 1, :], ACT.Ln, bias=1.0).then_inc(s.t_ln, 1)
                for g in range(4):
                    act.wait_ge(s.bc, g + 1)
                    act.copy(bcx[:, bass.ts(g, BANK)], m.bank[g][0:96, :]).then_inc(s.bcx, 1)
                act.wait_ge(s.bcx, 4)
                act.copy(m.bc3[:], bcx).then_inc(s.p1, 1)
                for k in range(KD):
                    act.wait_ge(s.sp, k + 1)
                    act.activation(m.lnd[:, k, :], m.lnd[:, k, :], ACT.Tanh, scale=1.0 / HALFSPAN, bias=m.eps[:, 2:3]).then_inc(s.th, 1)
                act.wait_ge(s.r1, 1)
                act.copy(p2, r1).then_inc(s.p2, 1)
                for k in range(KD):
                    act.wait_ge(s.delta, k + 1)
                    act.activation(m.lnd[:, k, :], m.lnd[:, k, :], ACT.Ln).then_inc(s.lnd, 1)
                for k in range(KD):
                    act.wait_ge(s.lnd, k + 1)
                    act.activation(t1[:, k, :], m.lnd[:, k, :], ACT.Exp, scale=0.5).then_inc(s.sq, 1)
                for n in range(8):
                    g, k = n // KD, n % KD
                    act.wait_ge(s.turned, 8 + n + 1)
                    act.copy(m.x0T[:, k, bass.ts(g, BANK)], m.bank[4 + n % 4][:, :]).then_inc(s.evac_a, 1)

            @block.tensor
            def _(pe):
                for g in range(4):
                    pe.wait_ge(s.xr, 4 * g + 4)
                    for k in range(KD):
                        for q in range(4):
                            t = pe.transpose(m.bank[g * KD + k][:, bass.ts(q, P)], xr[:, 4 * g + q, bass.ts(k, P)], m.ident[:])
                        t.then_inc(s.turned, 1)
                for j in range(8):
                    k, g = j // 4, j % 4
                    pe.wait_ge(s.evac_d, max(KD * (g + 1), j + 1))
                    for c in range(KD):
                        mm = pe.matmul(m.bank[j][:, :], m.wd[:, c, bass.ts(k, P)], m.xrT[:, c, bass.ts(g, BANK)],
                                       start=(c == 0), stop=(c == KD - 1))
                    mm.then_inc(s.z, 1)
                for g in range(4):
                    pe.wait_ge(s.zb, g + 1)
                    for c in range(KD):
                        mm = pe.matmul(m.bank[g][0:96, :], m.wbc[:, c, :], m.xrT[:, c, bass.ts(g, BANK)],
                                       start=(c == 0), stop=(c == KD - 1))
                    mm.then_inc(s.bc, 1)
                for n in range(8):
                    g, k = n // KD, n % KD
                    pe.wait_ge(s.x0, 4 * g + 4)
                    if n < 4:
                        pe.wait_ge(s.zb, 4 + n + 1)
                    else:
                        pe.wait_ge(s.evac_a, n - 3)
                    for q in range(4):
                        t = pe.transpose(m.bank[4 + n % 4][:, bass.ts(q, P)], x0[:, 4 * g + q, bass.ts(k, P)], m.ident[:])
                    t.then_inc(s.turned, 1)
        s.clear()


def scan_half(nc, half, m):
    with ExitStack() as ctx:
        s = stage_sems(nc, ctx, f"scan{half}", "bc_psum bc_sbuf inv decay w bx h hc y_added carried y_out")
        work = lambda n: m.work[:, bass.ts(n, HALF)]
        Bs, Cs = [work(0), work(1)], [work(2), work(3)]
        inv, dec, w, bx, h, hc = ([work(4 + 2 * n), work(5 + 2 * n)] for n in range(6))
        y = [m.pair[0], m.pair[1]]
        pB, pC = m.pair[2], m.pair[3]
        t0 = half * HALF
        last = NS - 1
        with nc.Block() as block:

            @block.tensor
            def _(pe):
                def spread(n, it):
                    pe.wait_ge(s.bc_sbuf, 2 * it)
                    for dst, row in ((pB, n), (pC, n + NS)):
                        for q in range(2):
                            mm = pe.matmul(dst[:, q, :], m.sel[:, bass.ts(row, P)], m.bc3[:, t0 + BANK * q:t0 + BANK * (q + 1)],
                                           start=True, stop=True)
                        mm.then_inc(s.bc_psum, 1)

                def add(it):
                    for k in range(KD):
                        pe.wait_ge(s.hc, 2 * it + k + 1)
                        for q in range(2):
                            mm = pe.matmul(y[k][:, q, :], m.ident[:], hc[k][:, bass.ts(q, BANK)],
                                           start=False, stop=True, skip_group_check=True)
                        mm.then_inc(s.y_added, 1)

                for dst, row in ((pB, 0), (pC, NS)):
                    for q in range(2):
                        mm = pe.matmul(dst[:, q, :], m.sel[:, bass.ts(row, P)], m.bc3[:, t0 + BANK * q:t0 + BANK * (q + 1)],
                                       start=True, stop=True)
                    mm.then_inc(s.bc_psum, 1)
                for k in range(KD):
                    for q in range(2):
                        pe.matmul(y[k][:, q, :], m.dskip[:, k, :], m.xrT[:, k, t0 + BANK * q:t0 + BANK * (q + 1)],
                                  start=True, stop=True)
                spread(1, 1)
                with pe.Fori(0, NS - 2) as n:
                    spread(n + 2, n + 2)
                    add(n)
                add(NS - 2)
                add(NS - 1)

            @block.scalar
            def _(act):
                def bc_out(it, j):
                    act.wait_ge(s.bc_psum, 2 * it + 1)
                    act.wait_ge(s.w, 2 * it - 2)
                    act.copy(Bs[j], pB[:].rearrange("p a b -> p (a b)")).then_inc(s.bc_sbuf, 1)
                    act.wait_ge(s.bc_psum, 2 * it + 2)
                    act.wait_ge(s.hc, 2 * it - 2)
                    act.copy(Cs[j], pC[:].rearrange("p a b -> p (a b)")).then_inc(s.bc_sbuf, 1)

                def decays(n, it, first=False):
                    for k in range(KD):
                        if not first:
                            act.wait_ge(s.bx, 2 * it - 1 + k)
                        act.activation(inv[k], m.lnd[:, k, t0:t0 + HALF], ACT.Sigmoid, scale=-1.0,
                                       bias=m.ainv[:, k, bass.ds(n, 1)]).then_inc(s.inv, 1)
                        if not first:
                            act.wait_ge(s.h, 2 * it - 1 + k)
                        act.activation(dec[k], m.lnd[:, k, t0:t0 + HALF], ACT.Tanh, scale=-0.5,
                                       bias=m.adec[:, k, bass.ds(n, 1)]).then_inc(s.decay, 1)

                for it in range(2):
                    act.wait_ge(s.bc_psum, 2 * it + 1)
                    act.copy(Bs[it], pB[:].rearrange("p a b -> p (a b)")).then_inc(s.bc_sbuf, 1)
                    act.wait_ge(s.bc_psum, 2 * it + 2)
                    act.copy(Cs[it], pC[:].rearrange("p a b -> p (a b)")).then_inc(s.bc_sbuf, 1)
                    decays(it, it, first=(it == 0))
                with act.Fori(1, NS // 2) as pair:
                    for j in range(2):
                        bc_out(2 * pair + j, j)
                        decays(2 * pair + j, 2 * pair + j)
                act.wait_ge(s.y_added, 2 * NS)
                for k in range(KD):
                    act.copy(m.sT[:, k, t0:t0 + HALF], y[k][:].rearrange("p a b -> p (a b)")).then_inc(s.y_out, 1)

            @block.gpsimd
            def _(pool):
                def inputs(it, j, first=False):
                    for k in range(KD):
                        pool.wait_ge(s.bc_sbuf, 2 * it + 1)
                        if not first:
                            pool.wait_ge(s.bx, 2 * it - 1 + k)
                        pool.tensor_tensor(w[k], m.u[:, k, t0:t0 + HALF], Bs[j], ALU.mult).then_inc(s.w, 1)

                def carry(n, it):
                    if half:
                        return
                    for k in range(KD):
                        pool.wait_ge(s.h, 2 * it + k + 1)
                        pool.tensor_copy(m.carry[:, k, bass.ds(n, 1)], h[k][:, HALF - 1:HALF]).then_inc(s.carried, 1)

                inputs(0, 0, first=True)
                inputs(1, 1)
                carry(0, 0)
                with pool.Fori(1, NS // 2) as pair:
                    for j in range(2):
                        it = 2 * pair + j
                        inputs(it, j)
                        carry(it - 1, it - 1)
                carry(last, last)

            @block.vector
            def _(dve):
                def step(n, it, j, first=False):
                    for k in range(KD):
                        dve.wait_ge(s.inv, 2 * it + k + 1)
                        dve.wait_ge(s.w, 2 * it + k + 1)
                        if not first:
                            dve.wait_ge(s.h, 2 * it - 1 + k)
                        dve.tensor_tensor(bx[k], w[k], inv[k], ALU.mult).then_inc(s.bx, 1)
                    for k in range(KD):
                        dve.wait_ge(s.bx, 2 * it + k + 1)
                        dve.wait_ge(s.decay, 2 * it + k + 1)
                        if not first:
                            dve.wait_ge(s.hc, 2 * it - 1 + k)
                            if not half:
                                dve.wait_ge(s.carried, 2 * it - 1 + k)
                        dve.tensor_tensor_scan(h[k], dec[k], bx[k], m.carry[:, k, bass.ds(n, 1)] if half else 0.0,
                                               ALU.mult, ALU.add).then_inc(s.h, 1)
                    for k in range(KD):
                        dve.wait_ge(s.h, 2 * it + k + 1)
                        dve.wait_ge(s.bc_sbuf, 2 * it + 2)
                        if not first:
                            dve.wait_ge(s.y_added, 2 * it - 1 + k)
                        dve.tensor_tensor(hc[k], h[k], Cs[j], ALU.mult).then_inc(s.hc, 1)

                step(0, 0, 0, first=True)
                step(1, 1, 1)
                with dve.Fori(1, NS // 2) as pair:
                    for j in range(2):
                        step(2 * pair + j, 2 * pair + j, j)
        s.clear()


def routed_expert(nc, e, m):
    with ExitStack() as ctx:
        s = stage_sems(nc, ctx, "routed", "hid relu sq out acc")
        relu = [m.work[:, bass.ts(n, BANK)] for n in range(4)]
        sq = [m.work[:, bass.ts(n, BANK)] for n in range(4, 8)]
        with nc.Block() as block:

            @block.tensor
            def _(pe):
                for g in range(4):
                    for c in range(KD):
                        mm = pe.matmul(m.bank[g][:, :], m.w1[:, c, :], m.x0T[:, c, bass.ts(g, BANK)],
                                       start=(c == 0), stop=(c == KD - 1))
                    mm.then_inc(s.hid, 1)
                for i in range(TILES):
                    pe.wait_ge(s.sq, i // 4 + 1)
                    if i >= 4:
                        pe.wait_ge(s.acc, i - 3)
                    pe.matmul(m.bank[4 + i % 4][:, 0:D], sq[i // 4][:, bass.ts(i % 4, P)], m.w2[:],
                              start=True, stop=True).then_inc(s.out, 1)

            @block.scalar
            def _(act):
                for g in range(4):
                    act.wait_ge(s.hid, g + 1)
                    act.activation(relu[g], m.bank[g][:, :], ACT.Relu).then_inc(s.relu, 1)
                    act.wait_ge(s.relu, g + 1)
                    act.activation(sq[g], relu[g], ACT.Square).then_inc(s.sq, 1)

            @block.vector
            def _(dve):
                for i in range(TILES):
                    dve.wait_ge(s.out, i + 1)
                    dve.scalar_tensor_tensor(m.nat[:, i, :], m.bank[4 + i % 4][:, 0:D], m.prob[:, i, bass.ds(e, 1)],
                                             m.nat[:, i, :], ALU.mult, ALU.add).then_inc(s.acc, 1)
        s.clear()


def shared_expert(nc, m):
    with ExitStack() as ctx:
        s = stage_sems(nc, ctx, "shared", "logit top diff ex s1 s2 prob pmax count flag hid relu sq out acc")
        lg, top, t = m.lg, m.top, m.small
        relu = [m.work[:, bass.ts(n, BANK)] for n in range(4)]
        sq = [m.work[:, bass.ts(n, BANK)] for n in range(4, 8)]
        with nc.Block() as block:

            @block.tensor
            def _(pe):
                for i in range(TILES):
                    for c in range(KD):
                        mm = pe.matmul(m.bank[2][:, bass.ts(i, E0)], m.x0T[:, c, bass.ts(i, P)], m.wr[:, c, :],
                                       start=(c == 0), stop=(c == KD - 1))
                mm.then_inc(s.logit, 1)
                for g in range(4):
                    if g >= 2:
                        pe.wait_ge(s.relu, g - 1)
                    for c in range(KD):
                        mm = pe.matmul(m.bank[g % 2], m.ws1[:, c, :], m.x0T[:, c, bass.ts(g, BANK)],
                                       start=(c == 0), stop=(c == KD - 1))
                    mm.then_inc(s.hid, 1)
                for i in range(TILES):
                    pe.wait_ge(s.sq, i // 4 + 1)
                    if i >= 4:
                        pe.wait_ge(s.acc, i - 3)
                    pe.matmul(m.bank[4 + i % 4][:, 0:D], sq[i // 4][:, bass.ts(i % 4, P)], m.ws2,
                              start=True, stop=True).then_inc(s.out, 1)
                pe.wait_ge(s.pmax, 1)
                pe.matmul(m.bank[3][0:1, 0:1], m.pmax, m.ones[:, 0:1], start=True, stop=True).then_inc(s.count, 1)

            @block.vector
            def _(dve):
                dve.wait_ge(s.logit, 1)
                dve.tensor_copy(lg[:].rearrange("p i e -> p (i e)"), m.bank[2][:, 0:TILES * E0]).then_inc(s.top, 1)
                dve.wait_ge(s.top, 1)
                for i in range(TILES):
                    dve.max(top[:, i, :], lg[:, i, :]).then_inc(s.top, 1)
                dve.wait_ge(s.top, 1 + TILES)
                dve.tensor_tensor(t[:, 0, :], top[:, :, 1], top[:, :, 0], ALU.subtract).then_inc(s.diff, 1)
                dve.wait_ge(s.ex, 1)
                dve.tensor_scalar(t[:, 2, :], t[:, 1, :], 1.0, None, ALU.add).then_inc(s.s1, 1)
                dve.wait_ge(s.s1, 1)
                dve.tensor_scalar(t[:, 3, :], t[:, 2, :], 1.0, None, ALU.is_equal).then_inc(s.s2, 1)
                for i in range(TILES):
                    dve.wait_ge(s.s2, 1)
                    dve.tensor_scalar(m.prob[:, i, :], lg[:, i, :], top[:, i, 0:1], t[:, 3, i:i + 1],
                                      ALU.is_equal, ALU.mult).then_inc(s.prob, 1)
                dve.wait_ge(s.prob, TILES)
                dve.tensor_reduce(m.pmax, m.prob.rearrange("p i e -> p (i e)"), AX_X, ALU.max).then_inc(s.pmax, 1)
                for i in range(TILES):
                    dve.wait_ge(s.out, i + 1)
                    dve.tensor_copy(m.nat[:, i, :], m.bank[4 + i % 4][:, 0:D]).then_inc(s.acc, 1)
                dve.wait_ge(s.count, 1)
                dve.tensor_copy(m.taken, m.bank[3][0:1, 0:1]).then_inc(s.flag, 1)

            @block.scalar
            def _(act):
                act.wait_ge(s.diff, 1)
                act.activation(t[:, 1, :], t[:, 0, :], ACT.Exp).then_inc(s.ex, 1)
                for g in range(4):
                    act.wait_ge(s.hid, g + 1)
                    act.activation(relu[g], m.bank[g % 2], ACT.Relu).then_inc(s.relu, 1)
                    act.wait_ge(s.relu, g + 1)
                    act.activation(sq[g], relu[g], ACT.Square).then_inc(s.sq, 1)
        s.clear()


def load_expert(nc, w1, w2, m):
    with ExitStack() as ctx:
        s = stage_sems(nc, ctx, "load_expert", "w_in")
        with nc.Block() as block:

            @block.sync
            def _(sp):
                sp.dma_start(m.w1[:], w1.rearrange("(c p) f -> p c f", p=P)).then_inc(s.w_in, 16)
                sp.dma_start(m.w2[:], w2).then_inc(s.w_in, 16)
                sp.wait_ge(s.w_in, 32)
        s.clear()


def finish_batch(nc, b, io, m):
    with ExitStack() as ctx:
        s = stage_sems(nc, ctx, "finish_batch", "turned sig silu g x1 stats mv root rstd xn turned2 evac stored")
        sig = m.work[:, 0:4096].rearrange("p (i d) -> p i d", i=TILES)
        xn = m.work[:, 4096:8192].rearrange("p (i d) -> p i d", i=TILES)
        stats, mv, sm = m.stats, m.mv, m.small
        with nc.Block() as block:

            @block.scalar
            def _(act):
                for g in range(4):
                    act.activation(sig[:, bass.ts(g, 4), :], m.nat[:, bass.ts(g, 4), :], ACT.Sigmoid).then_inc(s.sig, 1)

                def evac(g):
                    for k in range(KD):
                        act.wait_ge(s.turned2, g * KD + k + 1)
                        act.copy(m.x0T[:, k, bass.ts(g, BANK)], m.bank[g * KD + k][:, :]).then_inc(s.evac, 1)

                for g in range(4):
                    act.wait_ge(s.mv, 4 * (g + 1))
                    act.activation(sm[:, 0, bass.ts(g, 4)], mv[:, bass.ts(g, 4), 1], ACT.Sqrt, bias=m.eps[:, 0:1]).then_inc(s.root, 1)
                    if g == 3:
                        evac(0)
                for g in range(1, 4):
                    evac(g)

            @block.gpsimd
            def _(pool):
                for g in range(4):
                    four = bass.ts(g, 4)
                    pool.wait_ge(s.sig, g + 1)
                    pool.tensor_tensor(sig[:, four, :], sig[:, four, :], m.nat[:, four, :], ALU.mult).then_inc(s.silu, 1)

            @block.tensor
            def _(pe):
                for i in range(TILES):
                    if i >= 8:
                        pe.wait_ge(s.g, i - 7)
                    for k in range(KD):
                        t = pe.transpose(m.bank[i % 8][:, bass.ts(k, P)], m.sT[:, k, bass.ts(i, P)], m.ident[:])
                    t.then_inc(s.turned, 1)
                for g in range(4):
                    pe.wait_ge(s.xn, 4 * g + 4)
                    for k in range(KD):
                        pe.wait_ge(s.g, 8 + g * KD + k + 1)
                        for q in range(4):
                            t = pe.transpose(m.bank[g * KD + k][:, bass.ts(q, P)], xn[:, 4 * g + q, bass.ts(k, P)], m.ident[:])
                        t.then_inc(s.turned2, 1)

            @block.vector
            def _(dve):
                def sums(g):
                    dve.wait_ge(s.silu, g + 1)
                    for i in range(4 * g, 4 * g + 4):
                        dve.wait_ge(s.turned, i + 1)
                        dve.tensor_tensor(sig[:, i, :], sig[:, i, :], m.bank[i % 8][:, 0:D], ALU.mult).then_inc(s.g, 1)
                    for i in range(4 * g, 4 * g + 4):
                        dve.wait_ge(s.g, i + 1)
                        dve.tensor_tensor(m.x[:, i, :], m.x[:, i, :], sig[:, i, :], ALU.add).then_inc(s.x1, 1)
                    for i in range(4 * g, 4 * g + 4):
                        dve.wait_ge(s.x1, i + 1)
                        dve.bn_stats(stats[:, i, :], m.x[:, i, :]).then_inc(s.stats, 1)
                    for i in range(4 * g, 4 * g + 4):
                        dve.wait_ge(s.stats, i + 1)
                        dve.bn_aggr(mv[:, i, :], stats[:, i, :]).then_inc(s.mv, 1)

                def norm(g):
                    dve.wait_ge(s.root, g + 1)
                    dve.reciprocal(sm[:, 1, bass.ts(g, 4)], sm[:, 0, bass.ts(g, 4)]).then_inc(s.rstd, 1)
                    dve.wait_ge(s.rstd, g + 1)
                    for i in range(4 * g, 4 * g + 4):
                        dve.wait_ge(s.mv, i + 1)
                        dve.tensor_scalar(xn[:, i, :], m.x[:, i, :], mv[:, i, 0:1], sm[:, 1, i:i + 1],
                                          ALU.subtract, ALU.mult).then_inc(s.xn, 1)

                for g in range(4):
                    sums(g)
                    if g:
                        norm(g - 1)
                norm(3)

            @block.sync
            def _(sp):
                x1 = io.x1[bass.ts(b, 1), :, :].rearrange("o (i p) d -> p (o i) d", p=P)
                out = io.xn[bass.ts(b, 1), :, :].rearrange("o (i p) d -> p (o i) d", p=P)
                for g in range(2):
                    rows = bass.ts(g, 8)
                    sp.wait_ge(s.x1, 8 * (g + 1))
                    sp.dma_start(x1[:, rows, :], m.x[:, rows, :]).then_inc(s.stored, 16)
                    sp.wait_ge(s.xn, 8 * (g + 1))
                    sp.dma_start(out[:, rows, :], xn[:, rows, :]).then_inc(s.stored, 16)
                for g in range(2):
                    sp.wait_ge(s.evac, 4 * (g + 1))
                    for k in range(KD):
                        sp.dma_start(io.xnT[bass.ts(b, 1), k, :, bass.ts(g, 2 * BANK)].rearrange("o p t -> p (o t)"),
                                     m.x0T[:, k, bass.ts(g, 2 * BANK)]).then_inc(s.stored, 16)
                sp.wait_ge(s.stored, 16 * 8)
        s.clear()


def build_first_layer(nc, io):
    with ExitStack() as ctx:
        t = {}

        def sb(name, shape, dt=F32):
            made = ctx.enter_context(nc.sbuf_tensor("l0_" + name, shape, dt))
            t[name] = made[:]
        sb("x", [P, TILES, D])
        sb("nat", [P, TILES, D])
        sb("x0T", [P, KD, L])
        sb("xrT", [P, KD, L])
        sb("lnd", [P, KD, L])
        sb("u", [P, KD, L])
        sb("sT", [P, KD, L])
        sb("work", [P, 16 * HALF])
        sb("bc3", [96, L], BF16)
        sb("sel", [96, 2 * NS * P], BF16)
        sb("ident", [P, P])
        sb("dskip", [P, KD, P])
        sb("wd", [P, KD, D])
        sb("wbc", [P, KD, 96])
        sb("wr", [P, KD, E0])
        sb("w1", [P, KD, F0])
        sb("w2", [P, D])
        sb("ws1", [P, KD, F0]); sb("ws2", [P, D])
        sb("nw", [P, KD]); sb("bd", [P, KD]); sb("ds", [P, KD])
        sb("alog", [P, KD, NS]); sb("ainv", [P, KD, NS]); sb("adec", [P, KD, NS])
        sb("carry", [P, KD, NS])
        sb("stats", [P, TILES, 6]); sb("mv", [P, TILES, 2]); sb("small", [P, 6, TILES])
        sb("lg", [P, TILES, E0]); sb("top", [P, TILES, 8]); sb("prob", [P, TILES, E0])
        sb("eps", [P, 4]); sb("ones", [P, P]); sb("zero", [P, D]); sb("pmax", [P, 1]); sb("taken", [1, 1], I32)
        m = named(**t)
        s = stage_sems(nc, ctx, "build_first_layer", "w_in")
        with ExitStack() as c2:
            with nc.Block() as block:

                @block.sync
                def _(sp):
                    cols = [(m.wd, io.W_delta.rearrange("(c p) n -> p c n", p=P)), (m.wr, io.Wr.rearrange("(c p) n -> p c n", p=P)),
                            (m.alog, io.A_log.rearrange("(c p) n -> p c n", p=P)), (m.ident, io.ident), (m.sel, io.sel),
                            (m.ws1, io.Ws1.rearrange("(c p) f -> p c f", p=P)), (m.ws2, io.Ws2)]
                    for r in range(3):
                        cols.append((m.wbc[:, :, 32 * r:32 * r + NS], io.W_B.rearrange("(c p) n -> p c n", p=P)))
                        cols.append((m.wbc[:, :, 32 * r + NS:32 * r + 32], io.W_C.rearrange("(c p) n -> p c n", p=P)))
                    with nc.allow_non_contiguous_dma(reason="three columns of 128 numbers"):
                        for t, v in ((m.nw, io.norm_weight), (m.bd, io.b_delta), (m.ds, io.D_skip)):
                            sp.dma_start(t, v.rearrange("(c p) -> p c", p=P)).then_inc(s.w_in, 16)
                        for t, v in cols:
                            sp.dma_start(t, v).then_inc(s.w_in, 16)
                    sp.wait_ge(s.w_in, 16 * (3 + len(cols)))

                @block.vector
                def _(dve):
                    dve.memset(m.ones, 1.0)
                    dve.memset(m.zero, 0.0)
                    dve.memset(m.eps[:, 0:1], LN_EPS)
                    dve.memset(m.eps[:, 1:2], RMS_EPS)
                    dve.memset(m.eps[:, 2:3], -CENTER / HALFSPAN)
                    dve.wait_ge(s.w_in, 16 * 16)
                    for k in range(KD):
                        dve.tensor_scalar(m.dskip[:, k, :], m.ident[:], m.ds[:, k:k + 1], None, ALU.mult)
                    dve.tensor_scalar(m.ainv[:], m.alog[:], -1.0, LN2, ALU.mult, ALU.add)
                    dve.tensor_scalar(m.adec[:], m.alog[:], -0.5, LN2 / 2, ALU.mult, ALU.add)
        s.clear()
        ps = ctx.enter_context(nc.psum_tensor("l0_ps", [P, 8, BANK], F32))
        t["bank"] = [ps[:, i, :] for i in range(8)]
        t["pair"] = [ps[:, 2 * i:2 * i + 2, :] for i in range(4)]
        m = named(**t)
        with nc.Fori(0, B) as b:
            prepare_batch(nc, b, io, m)
            scan_half(nc, 0, m)
            scan_half(nc, 1, m)
            shared_expert(nc, m)
            taken = nc.values_load(m.taken, min_val=0, max_val=P)
            with nc.If(taken > 0):
                with nc.Fori(0, E0) as e:
                    load_expert(nc, io.W1[bass.ts(e, 1), :, :].rearrange("o d f -> (o d) f"),
                                io.W2[bass.ts(e, 1), :, :].rearrange("o f d -> (o f) d"), m)
                    routed_expert(nc, e, m)
            finish_batch(nc, b, io, m)



E1, I1 = 8, 512
CAP = int(T * 2 * 1.25 / E1)
SLOTS = E1 * CAP
ROWS = 512
BLOCKS = CAP // ROWS
FAR = float(1 << 20)


def route_batch(nc, b, j, io, m):
    with ExitStack() as ctx:
        s = stage_sems(nc, ctx, f"route{j}", "xt_in x_in logit lg top idx chain counts base_ok gates kept")
        lg, top, idx, fidx = m.lg, m.top, m.idx, m.fidx
        oh, pos, base, tmp = m.oh, m.pos, m.base, m.tmp
        with nc.Block() as block:

            @block.sync
            def _(sp):
                for k in range(KD):
                    sp.dma_start(m.xT[:, k, :], io.xnT[bass.ts(b, 1), k, :, :].rearrange("o p t -> p (o t)")).then_inc(s.xt_in, 16)
                sp.dma_start(m.xn[:, j, :, :], io.xn[bass.ts(b, 1), :, :].rearrange("o (i p) d -> p (o i) d", p=P)).then_inc(s.x_in, 16)
                sp.wait_ge(s.x_in, 16)
                sp.wait_ge(s.gates, 4)
                sp.dma_start(io.places[bass.ts(b, 1), :, :, :].rearrange("o p k i -> (o p) k i"), m.gidx).then_inc(s.kept, 16)
                sp.dma_start(io.gates[bass.ts(b, 1), :, :, :].rearrange("o p k i -> (o p) k i"), m.gate).then_inc(s.kept, 16)
                sp.wait_ge(s.kept, 32)

            @block.tensor
            def _(pe):
                pe.wait_ge(s.xt_in, 32)
                for i in range(TILES):
                    for c in range(KD):
                        mm = pe.matmul(m.bank[0][:, bass.ts(i, E1)], m.xT[:, c, bass.ts(i, P)], m.wg[:, c, :],
                                       start=(c == 0), stop=(c == KD - 1))
                mm.then_inc(s.logit, 1)
                pe.wait_ge(s.chain, 3)
                pe.matmul(m.bank[1][:, 0:TILES * E1], m.before, oh[:, 2, :, :].rearrange("p i e -> p (i e)"), start=True, stop=True)
                pe.matmul(m.bank[2][:, 0:TILES * E1], m.ones, oh[:, 2, :, :].rearrange("p i e -> p (i e)"), start=True, stop=True).then_inc(s.counts, 1)

            @block.vector
            def _(dve):
                n = [0]

                def then(ins):
                    n[0] += 1
                    ins.then_inc(s.chain, 1)
                    dve.wait_ge(s.chain, n[0])

                dve.wait_ge(s.logit, 1)
                dve.tensor_copy(lg.rearrange("p i e -> p (i e)"), m.bank[0][:, 0:TILES * E1]).then_inc(s.lg, 1)
                dve.wait_ge(s.lg, 1)
                for i in range(TILES):
                    dve.max(top[:, i, :], lg[:, i, :]).then_inc(s.top, 1)
                for i in range(TILES):
                    dve.wait_ge(s.top, i + 1)
                    dve.max_index(idx[:, i, :], top[:, i, :], lg[:, i, :]).then_inc(s.idx, 1)
                dve.wait_ge(s.idx, TILES)
                for k in range(2):
                    dve.tensor_copy(fidx[:, k, :], idx[:, :, k]).then_inc(s.lg, 1)
                dve.wait_ge(s.lg, 3)
                for k in range(2):
                    then(dve.tensor_tensor(oh[:, k, :, :], m.eid.unsqueeze(1).to_broadcast([P, TILES, E1]),
                                           fidx[:, k, :].unsqueeze(2).to_broadcast([P, TILES, E1]), ALU.is_equal))
                then(dve.tensor_tensor(oh[:, 2, :, :], oh[:, 0, :, :], oh[:, 1, :, :], ALU.add))
                then(dve.tensor_copy(base[:, :, 0:1], base[:, :, TILES:TILES + 1]))
                dve.wait_ge(s.counts, 1)
                then(dve.tensor_copy(m.count.rearrange("p e i -> p i e"), m.bank[2][:, 0:TILES * E1].rearrange("p (i e) -> p i e", e=E1)))
                for e in range(E1):
                    dve.tensor_tensor_scan(base[:, e, 1:TILES + 1], m.ones[:, 0:TILES], m.count[:, e, :], base[:, e, 0:1],
                                           ALU.mult, ALU.add).then_inc(s.chain, 1)
                n[0] += E1
                dve.wait_ge(s.chain, n[0])
                then(dve.tensor_tensor(pos, base[:, :, 0:TILES].rearrange("p e i -> p i e"),
                                       m.bank[1][:, 0:TILES * E1].rearrange("p (i e) -> p i e", e=E1), ALU.add))
                for k in range(2):
                    place, keep, slot, near = (tmp[:, 4 * k + q, :] for q in range(4))
                    then(dve.tensor_tensor(oh[:, k, :, :], oh[:, k, :, :], pos, ALU.mult))
                    then(dve.tensor_reduce(place, oh[:, k, :, :], AX_X, ALU.add))
                    then(dve.tensor_scalar(keep, place, float(CAP), None, ALU.is_lt))
                    then(dve.scalar_tensor_tensor(slot, fidx[:, k, :], float(CAP), place, ALU.mult, ALU.add))
                    then(dve.scalar_tensor_tensor(slot, keep, -FAR, slot, ALU.mult, ALU.add))
                    then(dve.tensor_scalar(m.sidx[:, j, k, :], slot, FAR, None, ALU.add))
                    then(dve.tensor_scalar(near, place, float(CAP - 1), None, ALU.min))
                    then(dve.scalar_tensor_tensor(near, fidx[:, k, :], float(CAP), near, ALU.mult, ALU.add))
                    then(dve.tensor_copy(m.gidx[:, k, :], near))
                    ins = dve.tensor_tensor(m.diff[:, k, :], top[:, :, k], top[:, :, 1 - k], ALU.subtract)
                    then(ins)
                    ins = dve.sem_inc(s.base_ok, 1)
                    dve.wait_ge(s.gates, 2 * k + 1)
                    dve.tensor_tensor(m.gate[:, k, :], m.gate[:, k, :], keep, ALU.mult).then_inc(s.gates, 1)

            @block.scalar
            def _(act):
                for k in range(2):
                    act.wait_ge(s.base_ok, k + 1)
                    act.activation(m.gate[:, k, :], m.diff[:, k, :], ACT.Sigmoid).then_inc(s.gates, 1)

            @block.gpsimd
            def _(pool):
                scatter(pool, 1 - j, io, m)
                pool.wait_ge(m.scattered, (b + 1) * (16 * 2 * TILES))
        s.clear()


def scatter(pool, j, io, m):
    for k in range(2):
        for i in range(TILES):
            pool.indirect_dma_start(io.xd, bass.IndirectOffsetOnAxis(ap=m.sidx[:, j, k, i:i + 1], axis=0), m.xn[:, j, i, :], None,
                                    bounds_check=SLOTS - 1, oob_is_err=False).then_inc(m.scattered, 16)


def run_experts(nc, io, m):
    with ExitStack() as ctx:
        s = stage_sems(nc, ctx, "exp", "w0 w1 x0 x1 turned xt hid gelu prod out y st0 st1 wfree")
        wl, xl, st = (s.w0, s.w1), (s.x0, s.x1), (s.st0, s.st1)
        TURN, HID = [m.bank[0], m.bank[1]], [m.pair[1], m.pair[2]]
        Y = m.pair[3]
        T0, X0, H0, G0, O0, Y0, S0 = 4, 2, 8, 2, 4, 2, 16
        PER = 2 * BLOCKS

        with nc.Block() as block:

            @block.sync
            def _(sp):
                def weights(e, buf):
                    sp.dma_start(m.w1[:, buf, :, :], io.eW1[bass.ds(e, 1), :, :].rearrange("o (c p) f -> p (o c) f", p=P)).then_inc(wl[buf], 16)
                    sp.dma_start(m.w2[:, buf, :, :], io.eW2[bass.ds(e, 1), :, :].rearrange("o (c p) d -> p (o c) d", p=P)).then_inc(wl[buf], 16)

                def rows_out(n, c):
                    sp.wait_ge(s.y, 2 * n + 2 + Y0)
                    sp.dma_start(io.yd[bass.ds(n * ROWS, ROWS), :].rearrange("(i p) d -> p i d", p=P), m.yout[:, c % 2, :, :]).then_inc(st[c % 2], 16)

                weights(0, 0)
                sp.wait_ge(s.turned, T0)
                sp.dma_start(m.xin[:, 0, :, :], io.xd[0:ROWS, :].rearrange("(i p) d -> p i d", p=P)).then_inc(xl[0], 16)
                with sp.Fori(0, E1 // 2) as g:
                    for e in range(2):
                        sp.wait_ge(s.wfree, 2 * g + e + 1)
                        weights((2 * g + e + 1) % E1, 1 - e)
                        for c in range(e * BLOCKS, (e + 1) * BLOCKS):
                            n = PER * g + c
                            sp.wait_ge(s.turned, 2 * n + T0)
                            nxt = (n + 1) % (E1 * BLOCKS)
                            sp.dma_start(m.xin[:, (c + 1) % 2, :, :], io.xd[bass.ds(nxt * ROWS, ROWS), :].rearrange("(i p) d -> p i d", p=P)).then_inc(xl[(c + 1) % 2], 16)
                            rows_out(n, c)
                sp.wait_ge(st[0], 16 * E1 * BLOCKS // 2 + S0)
                sp.wait_ge(st[1], 16 * E1 * BLOCKS // 2 + S0)
                sp.wait_ge(xl[0], 16 * (E1 * BLOCKS // 2 + 1))
                sp.wait_ge(wl[0], 32 * (E1 // 2 + 1))

            @block.tensor
            def _(pe):
                pe.sem_inc(s.turned, T0)
                pe.sem_inc(s.hid, H0)
                pe.sem_inc(s.out, O0)
                pe.sem_inc(s.wfree, 1)

                def turn(n, c, loads):
                    pe.wait_ge(xl[c % 2], loads)
                    pe.wait_ge(s.xt, 2 * n - 2 + 2 + X0)
                    for k in range(KD):
                        for q in range(4):
                            t = pe.transpose(TURN[k][:, bass.ts(q, P)], m.xin[:, c % 2, q, bass.ts(k, P)], m.ident)
                        t.then_inc(s.turned, 1)

                def hidden(n, c, e, mt):
                    pe.wait_ge(s.prod, 4 * n + mt - 1 + G0)
                    for half in range(2):
                        for k in range(KD):
                            col = half * I1 + mt * P
                            mm = pe.matmul(HID[mt % 2][:, half, :], m.w1[:, e, k, col:col + P], m.xt[:, c % 2, k, :],
                                           start=(k == 0), stop=(k == KD - 1))
                    mm.then_inc(s.hid, 1)

                def outputs(n, c, e):
                    for k in range(4):
                        pe.wait_ge(s.prod, 4 * n + k + 1 + G0)
                        for r in range(4):
                            if k == 0 and r % 2 == 0:
                                pe.wait_ge(s.y, 2 * n + r // 2 - 1 + Y0)
                            mm = pe.matmul(Y[:, r // 2, (r % 2) * D:(r % 2 + 1) * D], m.ht[:, c % 2, k, bass.ts(r, P)], m.w2[:, e, k, :],
                                           start=(k == 0 and r % 2 == 0), stop=(k == 3), skip_group_check=True)
                            if k == 3 and r % 2:
                                mm.then_inc(s.out, 1)

                pe.wait_ge(xl[0], 16)
                for k in range(KD):
                    for q in range(4):
                        t = pe.transpose(TURN[k][:, bass.ts(q, P)], m.xin[:, 0, q, bass.ts(k, P)], m.ident)
                    t.then_inc(s.turned, 1)
                with pe.Fori(0, E1 // 2) as g:
                    for e in range(2):
                        pe.wait_ge(wl[e], 32 * (g + 1))
                        for c in range(e * BLOCKS, (e + 1) * BLOCKS):
                            n = PER * g + c
                            pe.wait_ge(s.xt, 2 * n + 2 + X0)
                            for mt in range(4):
                                hidden(n, c, e, mt)
                            turn(n + 1, c + 1, 16 * (BLOCKS * g + (c + 1) // 2 + 1))
                            outputs(n, c, e)
                        pe.sem_inc(s.wfree, 1)

            @block.scalar
            def _(act):
                act.sem_inc(s.xt, X0)

                def evac(n, c):
                    act.wait_ge(s.hid, 4 * n - 4 + H0)
                    for k in range(KD):
                        act.wait_ge(s.turned, 2 * n + k + 1 + T0)
                        act.copy(m.xt[:, c % 2, k, :], TURN[k]).then_inc(s.xt, 1)

                act.wait_ge(s.hid, H0)
                for k in range(KD):
                    act.wait_ge(s.turned, k + 1 + T0)
                    act.copy(m.xt[:, 0, k, :], TURN[k]).then_inc(s.xt, 1)
                with act.Fori(0, E1 // 2) as g:
                    for c in range(PER):
                        n = PER * g + c
                        for mt in range(4):
                            act.wait_ge(s.hid, 4 * n + mt + 1 + H0)
                            act.wait_ge(s.prod, 4 * n + mt - 1 + G0)
                            act.activation(m.g[:, mt % 2, :], HID[mt % 2][:, 0, :], ACT.Gelu).then_inc(s.gelu, 1)
                        evac(n + 1, c + 1)

            @block.vector
            def _(dve):
                dve.sem_inc(s.prod, G0)
                dve.sem_inc(s.y, Y0)
                dve.sem_inc(st[0], S0)
                dve.sem_inc(st[1], S0)
                with dve.Fori(0, E1 // 2) as g:
                    for c in range(PER):
                        n = PER * g + c
                        dve.wait_ge(s.out, 2 * n - 2 + O0)
                        for mt in range(4):
                            dve.wait_ge(s.gelu, 4 * n + mt + 1)
                            dve.tensor_tensor(m.ht[:, c % 2, mt, :], m.g[:, mt % 2, :], HID[mt % 2][:, 1, :], ALU.mult).then_inc(s.prod, 1)
                        dve.wait_ge(st[c % 2], 16 * (BLOCKS * g + c // 2) + S0)
                        for j in range(2):
                            dve.wait_ge(s.out, 2 * n + j + 1 + O0)
                            dve.tensor_copy(m.yout[:, c % 2, 2 * j:2 * j + 2, :].rearrange("p i d -> p (i d)"), Y[:, j, :]).then_inc(s.y, 1)
        s.clear()


def build_second_ffn(nc, io):
    with ExitStack() as ctx:
        t = {}

        def sb(name, shape, dt=F32, c=ctx):
            t[name] = c.enter_context(nc.sbuf_tensor("ff_" + name, shape, dt))[:]
        ps = ctx.enter_context(nc.psum_tensor("ff_ps", [P, 8, BANK], F32))
        t["bank"] = [ps[:, i, :] for i in range(8)]
        t["pair"] = [ps[:, 2 * i:2 * i + 2, :] for i in range(4)]
        sb("ident", [P, P])
        sb("gidx", [P, 2, TILES], U32); sb("gate", [P, 2, TILES])
        m = named(**t)
        with ExitStack() as c2:
            sb("xT", [P, KD, L], F32, c2); sb("xn", [P, 2, TILES, D], F32, c2)
            sb("wg", [P, KD, E1], F32, c2); sb("before", [P, P], F32, c2); sb("ones", [P, P], F32, c2)
            sb("eid", [P, E1], F32, c2); sb("count", [P, E1, TILES], F32, c2)
            sb("lg", [P, TILES, E1], F32, c2); sb("top", [P, TILES, 8], F32, c2); sb("idx", [P, TILES, 8], U32, c2)
            sb("fidx", [P, 2, TILES], F32, c2); sb("oh", [P, 3, TILES, E1], F32, c2); sb("pos", [P, TILES, E1], F32, c2)
            sb("base", [P, E1, TILES + 1], F32, c2); sb("tmp", [P, 8, TILES], F32, c2); sb("sidx", [P, 2, 2, TILES], U32, c2)
            sb("diff", [P, 2, TILES], F32, c2)
            m = named(**t)
            s = stage_sems(nc, c2, "ff_load", "w_in")
            with nc.Block() as block:

                @block.sync
                def _(sp):
                    for t, v in ((m.ident, io.ident), (m.wg, io.WgT.rearrange("(c p) n -> p c n", p=P)), (m.before, io.before),
                                 (m.eid, io.eid)):
                        sp.dma_start(t, v).then_inc(s.w_in, 16)
                    sp.wait_ge(s.w_in, 64)

                @block.vector
                def _(dve):
                    dve.memset(m.sidx[:, 1, :, :], int(FAR))
                    dve.memset(m.xn[:, 1, :, :], 0.0)
                    dve.memset(m.ones, 1.0)
                    dve.memset(m.base, 0.0)
            s.clear()
            t["scattered"] = c2.enter_context(nc.semaphore("scattered"))
            m = named(**t)
            with nc.Fori(0, B // 2) as pair:
                for j in range(2):
                    route_batch(nc, 2 * pair + j, j, io, m)
            with nc.Block() as block:

                @block.gpsimd
                def _(pool):
                    scatter(pool, 1, io, m)
                    pool.wait_ge(m.scattered, (B + 1) * (16 * 2 * TILES))
        with ExitStack() as c2:
            sb("w1", [P, 2, KD, 2 * I1], F32, c2); sb("w2", [P, 2, 4, D], F32, c2)
            sb("xin", [P, 2, 4, D], F32, c2); sb("xt", [P, 2, KD, ROWS], F32, c2)
            sb("g", [P, 2, ROWS], F32, c2); sb("ht", [P, 2, 4, ROWS], F32, c2); sb("yout", [P, 2, 4, D], F32, c2)
            m = named(**t)
            run_experts(nc, io, m)




H1, HD = 16, 16
SCALE = HD ** -0.5
LAMBDA_INIT = 0.8
HEADS = B * H1
STACK = 6 * HD
QB = 1024
KT = L // P
FT = 4
PARTS_Q, PARTS_K = ((0, 3), (0, 2), (0, 1)), ((0, 3), (1, 2), (2, 1))


def project_batch(nc, b, io, m):
    with ExitStack() as ctx:
        s = stage_sems(nc, ctx, "project", "x0 x1 x2 x3 proj out p1 r1 p2 p3 v v_out stored")
        full, r1, parts = m.full, m.r1, (m.p1, m.p2, m.p3)
        UNITS = 2 * KD
        x_in = (s.x0, s.x1, s.x2, s.x3)
        with nc.Block() as block:

            @block.sync
            def _(sp):
                for g in range(4):
                    for k in range(KD):
                        sp.dma_start(m.xT[:, k, bass.ts(g, BANK)], io.xnT[bass.ts(b, 1), k, :, bass.ts(g, BANK)].rearrange("o p t -> p (o t)")).then_inc(x_in[g], 16)

                def store(u, part, done):
                    w, k = u // KD, u % KD
                    sp.wait_ge(done, u + 1)
                    v = (io.qp, io.kp)[w][bass.ts(b, 1), 8 * k:8 * k + 8, part, :, :].rearrange("o h d t -> (o h) d t")
                    sp.dma_start(v, parts[part][:, u, :]).then_inc(s.stored, 16)

                sp.wait_ge(s.v_out, TILES)
                sp.dma_start(io.vp[bass.ts(b, 1), :, :, :].rearrange("o h p t -> p (o h) t"),
                             m.v.rearrange("p h i c -> p h (i c)")).then_inc(s.stored, 16)
                for u in range(UNITS + 1):
                    if u < UNITS:
                        store(u, 0, s.p1)
                    if u:
                        store(u - 1, 1, s.p2)
                        store(u - 1, 2, s.p3)
                sp.wait_ge(s.stored, 16 * (1 + 3 * UNITS))

            @block.tensor
            def _(pe):
                for i in range(TILES):
                    if i % 4 == 0:
                        pe.wait_ge(x_in[i // 4], 32)
                    if i >= 8:
                        pe.wait_ge(s.v_out, i - 7)
                    for c in range(KD):
                        mm = pe.matmul(m.bank[i % 8][:, 0:D], m.xT[:, c, bass.ts(i, P)], m.wv[:, c, :],
                                       start=(c == 0), stop=(c == KD - 1))
                    mm.then_inc(s.v, 1)
                for u in range(UNITS):
                    w, k = u // KD, u % KD
                    for g in range(4):
                        n = 4 * u + g
                        if n < 8:
                            pe.wait_ge(s.v_out, TILES - 8 + n + 1)
                        else:
                            pe.wait_ge(s.out, n - 7)
                        for c in range(KD):
                            mm = pe.matmul(m.bank[n % 8], (m.wq, m.wk)[w][:, c, bass.ts(k, P)], m.xT[:, c, bass.ts(g, BANK)],
                                           start=(c == 0), stop=(c == KD - 1))
                        mm.then_inc(s.proj, 1)

            @block.scalar
            def _(act):
                for u in range(UNITS + 1):
                    if u < UNITS:
                        w, k = u // KD, u % KD
                        for g in range(4):
                            n = 4 * u + g
                            act.wait_ge(s.proj, n + 1)
                            act.activation(full[:, u, bass.ts(g, BANK)], m.bank[n % 8], ACT.Identity, bias=(m.bq, m.bk)[w][:, k:k + 1]).then_inc(s.out, 1)
                        act.wait_ge(s.out, 4 * (u + 1))
                        act.copy(m.p1[:, u, :], full[:, u, :]).then_inc(s.p1, 1)
                    if u:
                        act.wait_ge(s.r1, u)
                        act.copy(m.p2[:, u - 1, :], r1[:, u - 1, :]).then_inc(s.p2, 1)

            @block.vector
            def _(dve):
                for i in range(TILES):
                    dve.wait_ge(s.v, i + 1)
                    dve.tensor_tensor(m.v[:, :, i, 0:HD], m.bank[i % 8][:, 0:D].rearrange("p (h d) -> p h d", d=HD),
                                      m.bv.rearrange("p (h d) -> p h d", d=HD), ALU.add).then_inc(s.v_out, 1)
                for u in range(UNITS + 1):
                    if u < UNITS:
                        dve.wait_ge(s.p1, u + 1)
                        dve.tensor_tensor(r1[:, u, :], full[:, u, :], m.p1[:, u, :], ALU.subtract).then_inc(s.r1, 1)
                    if u:
                        dve.wait_ge(s.p2, u)
                        dve.wait_ge(s.r1, u)
                        dve.tensor_tensor(m.p3[:, u - 1, :], r1[:, u - 1, :], m.p2[:, u - 1, :], ALU.subtract).then_inc(s.p3, 1)
        s.clear()


def combine_experts(pool, io, m):
    PARTS = TILES // FT
    MOVED = 16 * (2 * FT + 1)
    pool.memset(m.units, 1.0).then_inc(m.gate_ready, 1)
    pool.wait_ge(m.gate_ready, 1)
    with pool.Fori(0, B) as b:
        pool.dma_start(m.gidx, io.places[bass.ts(b, 1), :, :, :].rearrange("o p k i -> (o p) k i")).then_inc(m.looked_up, 16)
        pool.dma_start(m.gate_in, io.gates[bass.ts(b, 1), :, :, :].rearrange("o p k i -> (o p) k i")).then_inc(m.looked_up, 16)
        pool.wait_ge(m.looked_up, 32 * (b + 1))
        pool.tensor_tensor(m.gate, m.gate_in, m.units, ALU.mult).then_inc(m.gate_ready, 1)
        for part in range(PARTS):
            done = PARTS * b + part
            for i in range(FT):
                for k in range(2):
                    place = m.gidx[:, k, FT * part + i:FT * part + i + 1]
                    pool.indirect_dma_start(m.y[:, k, i, :], None, io.yd, bass.IndirectOffsetOnAxis(ap=place, axis=0),
                                            bounds_check=SLOTS - 1, oob_is_err=False).then_inc(m.moved, 16)
            pool.wait_ge(m.gate_ready, b + 2)
            pool.wait_ge(m.moved, MOVED * done + 32 * FT)
            gates = m.gate[:, :, bass.ts(part, FT)].unsqueeze(3).to_broadcast([P, 2, FT, D])
            pool.tensor_tensor(m.y, m.y, gates, ALU.mult).then_inc(m.gated, 1)
            pool.wait_ge(m.gated, done + 1)
            pool.tensor_tensor(m.fsum, m.y[:, 0, :, :], m.y[:, 1, :, :], ALU.add).then_inc(m.summed, 1)
            pool.wait_ge(m.summed, done + 1)
            pool.dma_start(io.f[bass.ts(b, 1), :, part, :].rearrange("o p n -> (o p) n"),
                           m.fsum.rearrange("p i d -> p (i d)")).then_inc(m.moved, 16)
    pool.wait_ge(m.moved, MOVED * PARTS * B)


def attend(nc, io, m):
    with ExitStack() as ctx:
        s = stage_sems(nc, ctx, "att", "init loaded v_loaded score ex av o_copy o2 ring ring_free mfin mhi mlo mrow rec a_out")
        S, O, ring = [m.pair[0], m.pair[1]], m.pair[2], [m.bank[6], m.bank[7]]
        NRING = 34
        PRO = 65
        EX0, AV0, RF0 = 2, 4, 2
        ROUND, QUARTER, LAG = 4, 256, 6

        with nc.Block() as block:

            @block.sync
            def _(sp):
                def load(h, buf):
                    src_q, src_k = io.qp.rearrange("b h n d t -> (b h) n d t"), io.kp.rearrange("b h n d t -> (b h) n d t")
                    row = 0
                    for (q0, nq), (k0, nk) in zip(PARTS_Q, PARTS_K):
                        sp.dma_start(m.qs[row:row + HD * nq, buf, :],
                                     src_q[bass.ds(h, 1), q0:q0 + nq, :, :].rearrange("o n d t -> (o n d) t")).then_inc(s.loaded, 16)
                        for r in range(nq):
                            sp.dma_start(m.ks[row + HD * r:row + HD * (r + 1), buf, :],
                                         src_k[bass.ds(h, 1), k0, :, :].rearrange("o d t -> (o d) t")).then_inc(s.loaded, 16)
                        row += HD * nq

                def load_v(h, buf):
                    sp.dma_start(m.vst[:, buf, :, :], io.vp.rearrange("b h p t -> (b h) p t")[bass.ds(h, 1), :, :].rearrange("o p (i c) -> p (o i) c", c=32)).then_inc(s.v_loaded, 16)

                def rows(step, half, buf):
                    sp.wait_ge(s.mlo, step + 1)
                    for r in range(2):
                        sp.dma_start(m.qs[STACK + r:STACK + r + 1, buf, half * QB:(half + 1) * QB],
                                     m.mrow[:, r, :]).then_inc(s.mrow, 16)

                LOAD = 16 * 9
                sp.wait_ge(s.init, 3)
                load(0, 0)
                sp.wait_ge(s.loaded, LOAD)
                load(1, 1)
                load_v(0, 0)
                rows(0, 0, 0)
                with sp.Fori(0, HEADS // 4) as g:
                    for j in range(4):
                        h = 4 * g + j
                        sp.wait_ge(s.loaded, LOAD * (h + 2))
                        sp.wait_ge(s.score, 16 * (2 * h) + 1)
                        load((h + 2) % HEADS, (j + 2) % 4)
                        sp.wait_ge(s.v_loaded, 16 * (h + 1))
                        sp.wait_ge(s.av, 8 * (2 * h) + 3 + AV0)
                        load_v((h + 1) % HEADS, (j + 1) % 2)
                        rows(2 * h + 1, 1, j)
                        rows(2 * h + 2, 0, (j + 1) % 4)
                sp.wait_ge(s.loaded, LOAD * (HEADS + 2))
                sp.wait_ge(s.v_loaded, 16 * (HEADS + 1))
                sp.wait_ge(s.mrow, 32 * (2 * HEADS + 1))

            @block.gpsimd
            def _(pool):
                pool.memset(m.E[:, 8:16, :], 1.0).then_inc(s.init, 1)
                pool.wait_ge(s.init, 1)
                pool.memset(m.vst[:, 1, :, :], 1.0).then_inc(s.init, 1)
                pool.wait_ge(s.init, 2)
                pool.memset(m.ks[STACK:P, :, :], 1.0).then_inc(s.init, 1)
                pool.wait_ge(s.init, 3)
                combine_experts(pool, io, m)

            @block.tensor
            def _(pe):
                def peak(i, c, buf, n, wait):
                    pe.wait_ge(s.ring_free, wait)
                    pe.matmul(ring[n % 2], m.qs[0:STACK, buf, bass.ts(i, P)], m.ks[0:STACK, buf, bass.ts(c, BANK)],
                              start=True, stop=True).then_inc(s.ring, 1)

                def turn(n, wait, mf):
                    pe.wait_ge(s.mfin, mf)
                    pe.wait_ge(s.ring_free, wait)
                    pe.transpose(ring[n % 2][0:8, 0:P], m.mx[:], m.ident[:]).then_inc(s.ring, 1)

                def values(r, quarter, par):
                    cols = slice(QUARTER * (quarter % 2), QUARTER * (quarter % 2 + 1))
                    for q in range(ROUND):
                        kt = ROUND * r + q
                        mm = pe.matmul(O[32 * q:32 * q + 32, quarter // 2, cols], m.vst[:, par, kt, :], m.E[:, kt, bass.ts(quarter, QUARTER)],
                                       start=(r == 0 and quarter % 2 == 0), stop=(r == 3), skip_group_check=True)
                    if quarter % 2:
                        mm.then_inc(s.av, 1)

                def normalise(t, n, wait, t1):
                    pe.wait_ge(s.o_copy, t1)
                    pe.wait_ge(s.ring_free, wait)
                    for i in range(8):
                        mm = pe.matmul(ring[n % 2][:, 17 * i:17 * i + 17], m.osb[:, bass.ts(i, P)], m.selsum[:], start=True, stop=True)
                    mm.then_inc(s.ring, 1)

                LOAD = 16 * 9
                pe.wait_ge(s.init, 3)
                pe.wait_ge(s.loaded, LOAD)
                n = 0
                for half in range(2):
                    for i in range(8):
                        for c in range(4):
                            peak(8 * half + i, c, 0, n, n + 1)
                            n += 1
                    if half == 0:
                        turn(n, n + 1, 1)
                        n += 1
                assert n == PRO
                for q in range(ROUND):
                    for bank in range(2):
                        pe.matmul(O[32 * q:32 * q + 32, bank, :], m.vst[:, 1, q, :], m.E[:, 8 + q, bass.ts(bank, BANK)],
                                  start=True, stop=True, skip_group_check=True)

                def step(h, t, j, half):
                    local = 0
                    nxt = (j + 1) % 4

                    def w():
                        return PRO + NRING * t + local + 1
                    pe.wait_ge(s.mrow, 32 * (t + 1))
                    if half == 0:
                        pe.wait_ge(s.loaded, LOAD * (h + 2))
                        pe.wait_ge(s.v_loaded, 16 * (h + 1))
                    for kt in range(KT):
                        pe.wait_ge(s.ex, 16 * t + kt - 2 + 1 + EX0)
                        for hf in range(2):
                            mm = pe.matmul(S[kt % 2][:, hf, :], m.ks[0:STACK + 2, j, bass.ts(kt, P)],
                                           m.qs[0:STACK + 2, j, half * QB + hf * BANK:half * QB + (hf + 1) * BANK],
                                           start=True, stop=True)
                        mm.then_inc(s.score, 1)
                        peak(8 * half + kt // 2, 2 * kt % 4, nxt, PRO + local, w())
                        local += 1
                        if kt == 3:
                            turn(PRO + local, w(), t + 2)
                            local += 1
                        if kt == 9:
                            normalise(t, PRO + local, w(), 2 * t + 2)
                            local += 1
                        r, quarter = (kt - LAG) // ROUND % ROUND, (kt - LAG) % ROUND
                        if quarter == 0:
                            pe.wait_ge(s.ex, 16 * t + ROUND * ((kt - LAG) // ROUND + 1) + EX0)
                        if r == 0 and quarter % 2 == 0:
                            pe.wait_ge(s.o_copy, 2 * t + quarter // 2 + 1)
                        values(r, quarter, (j if half or kt >= LAG else j + 1) % 2)
                        peak(8 * half + kt // 2, 2 * kt % 4 + 1, nxt, PRO + local, w())
                        local += 1
                    assert local == NRING

                with pe.Fori(0, HEADS // 4) as g:
                    for j in range(4):
                        for half in range(2):
                            step(4 * g + j, 8 * g + 2 * j + half, j, half)
                t = 2 * HEADS
                pe.wait_ge(s.ex, 16 * t + EX0)
                for y in range(16 - LAG, 16):
                    values(y // ROUND, y % ROUND, (HEADS - 1) % 2)
                normalise(t, PRO, PRO + NRING * t + 1, 2 * t + 2)

            @block.scalar
            def _(act):
                act.sem_inc(s.ex, EX0)

                def copy_out(t, bank):
                    act.wait_ge(s.av, 8 * t + 2 + bank + AV0)
                    act.wait_ge(s.o2, t + 1)
                    act.copy(m.osb[:, bass.ts(bank, BANK)], O[:, bank, :]).then_inc(s.o_copy, 1)

                def step(t):
                    for kt in range(KT):
                        act.wait_ge(s.score, 16 * t + kt + 1)
                        if kt % ROUND == 0:
                            act.wait_ge(s.av, 8 * t + 2 * (kt // ROUND) - 3 + AV0)
                        act.activation(m.E[:, kt, :], S[kt % 2].rearrange("p a b -> p (a b)"), ACT.Exp, scale=SCALE).then_inc(s.ex, 1)
                        if kt in (3, 5):
                            copy_out(t, kt // 2 - 1)

                with act.Fori(0, HEADS) as h:
                    for half in range(2):
                        step(2 * h + half)
                copy_out(2 * HEADS, 0)
                copy_out(2 * HEADS, 1)

            @block.vector
            def _(dve):
                dve.sem_inc(s.ring_free, RF0)
                dve.sem_inc(s.av, AV0)
                dve.sem_inc(s.o2, 1)

                def peak(job, n, ready):
                    dve.wait_ge(s.ring, ready)
                    dve.tensor_reduce(m.mpart[:, job:job + 1], ring[n % 2], AX_X, ALU.max).then_inc(s.ring_free, 1)

                def last(t, ready):
                    dve.wait_ge(s.ring_free, ready + RF0)
                    dve.tensor_reduce(m.mx[:], m.mpart[:].rearrange("p (i c) -> p i c", c=4), AX_X, ALU.max).then_inc(s.mfin, 1)

                def turn(t, n, ready, rows_out):
                    dve.wait_ge(s.ring, ready)
                    if rows_out is not None:
                        dve.wait_ge(s.mrow, rows_out)
                    dve.tensor_scalar(m.mneg[:], ring[n % 2][0:8, 0:P], -1.0, None, ALU.mult).then_inc(s.ring_free, 1)
                    dve.wait_ge(s.ring_free, ready + RF0)
                    dve.tensor_copy(m.mrow[:, 0, :], m.mneg[:]).then_inc(s.mhi, 1)
                    dve.wait_ge(s.mhi, t + 1)
                    dve.tensor_tensor(m.mrow[:, 1, :], m.mneg[:], m.mrow[:, 0, :], ALU.subtract).then_inc(s.mlo, 1)

                def normalise(slot, half, t, n, ready):
                    dve.wait_ge(s.ring, ready)
                    o = ring[n % 2][:, 0:8 * 17].rearrange("p (i c) -> p i c", c=17)
                    dve.sem_inc(s.o2, 1)
                    dve.wait_ge(s.a_out, t + 1)
                    dve.reciprocal(m.rec[:], o[:, :, 16:17]).then_inc(s.rec, 1)
                    dve.wait_ge(s.rec, t + 1)
                    dve.tensor_tensor(m.A[:, bass.ds(slot, 1), 8 * half:8 * half + 8, :].rearrange("p o i d -> p (o i) d"),
                                      o[:, :, 0:HD], m.rec[:].to_broadcast([P, 8, HD]), ALU.mult).then_inc(s.a_out, 1)
                    dve.wait_ge(s.a_out, t + 2)
                    dve.sem_inc(s.ring_free, 1)

                dve.sem_inc(s.a_out, 1)
                n = 0
                for half in range(2):
                    if half:
                        dve.wait_ge(s.mfin, 1)
                    for i in range(32):
                        peak(i, n, n + 1)
                        n += 1
                    last(half, n)
                    if half == 0:
                        turn(0, n, n + 1, None)
                        n += 1

                def step(h, t, half):
                    local = 0
                    dve.wait_ge(s.mfin, t + 2)
                    for job in range(32):
                        peak(job, PRO + local, PRO + NRING * t + local + 1)
                        local += 1
                        if job == 6:
                            turn(t + 1, PRO + local, PRO + NRING * t + local + 1, 32 * (t + 1))
                            local += 1
                        if job == 18:
                            normalise(h + half, 1 - half, t, PRO + local, PRO + NRING * t + local + 1)
                            local += 1
                    last(t, PRO + NRING * t + local)

                with dve.Fori(0, HEADS) as h:
                    for half in range(2):
                        step(h, 2 * h + half, half)
                t = 2 * HEADS
                normalise(HEADS, 1, t, PRO, PRO + NRING * t + 1)
        s.clear()


def output_batch(nc, b, io, m):
    with ExitStack() as ctx:
        s = stage_sems(nc, ctx, "output", "f_in x_in mix turned evac out s_out sig silu prod sum stored")
        PARTS = TILES // FT
        with nc.Block() as block:

            @block.vector
            def _(dve):
                for g in range(PARTS):
                    for k in range(KD):
                        src = m.A[:, bass.ds(b * H1 + 1 + 8 * k, 8), :, :]
                        for i in range(FT * g, FT * (g + 1)):
                            dst = m.mix[:, i, bass.ts(k, P)].rearrange("p (h d) -> p h d", d=HD)
                            if k == 0:
                                x2 = m.A[:, bass.ds(b * H1 + 9, 8), :, :]
                                dve.scalar_tensor_tensor(dst, x2[:, :, i, :], m.nlam[:, 0:1], src[:, :, i, :],
                                                         ALU.mult, ALU.add).then_inc(s.mix, 1)
                            else:
                                dve.tensor_copy(dst, src[:, :, i, :]).then_inc(s.mix, 1)
                for g in range(PARTS):
                    tiles = bass.ts(g, FT)
                    for i in range(FT * g, FT * (g + 1)):
                        dve.wait_ge(s.out, i + 1)
                        dve.tensor_tensor(m.s[:, i, :], m.bank[i % 8][:, 0:D], m.bp[:], ALU.add).then_inc(s.s_out, 1)
                    dve.wait_ge(s.silu, g + 1)
                    dve.wait_ge(s.s_out, FT * (g + 1))
                    dve.tensor_tensor(m.s[:, tiles, :], m.s[:, tiles, :], m.f[:, tiles, :], ALU.mult).then_inc(s.prod, 1)

            @block.gpsimd
            def _(pool):
                for g in range(PARTS):
                    tiles = bass.ts(g, FT)
                    pool.wait_ge(s.sig, g + 1)
                    pool.tensor_tensor(m.f[:, tiles, :], m.f[:, tiles, :], m.sig[:, tiles, :], ALU.mult).then_inc(s.silu, 1)
                for g in range(PARTS):
                    tiles = bass.ts(g, FT)
                    pool.wait_ge(s.x_in, 16)
                    pool.wait_ge(s.prod, g + 1)
                    pool.tensor_tensor(m.x1[:, tiles, :], m.x1[:, tiles, :], m.s[:, tiles, :], ALU.add).then_inc(s.sum, 1)

            @block.tensor
            def _(pe):
                for g in range(4):
                    pe.wait_ge(s.mix, 2 * FT * (g + 1))
                    for k in range(KD):
                        for q in range(4):
                            t = pe.transpose(m.bank[g * KD + k][:, bass.ts(q, P)], m.mix[:, 4 * g + q, bass.ts(k, P)], m.ident[:])
                        t.then_inc(s.turned, 1)
                for i in range(TILES):
                    pe.wait_ge(s.evac, min(8, max(KD * (i // 4 + 1), i + 1)))
                    if i >= 8:
                        pe.wait_ge(s.s_out, i - 7)
                    for c in range(KD):
                        mm = pe.matmul(m.bank[i % 8][:, 0:D], m.outT[:, c, bass.ts(i, P)], m.wp[:, c, :],
                                       start=(c == 0), stop=(c == KD - 1))
                    mm.then_inc(s.out, 1)

            @block.scalar
            def _(act):
                act.wait_ge(s.f_in, 16)
                for g in range(PARTS):
                    tiles = bass.ts(g, FT)
                    act.activation(m.sig[:, tiles, :], m.f[:, tiles, :], ACT.Sigmoid).then_inc(s.sig, 1)
                for g in range(4):
                    for k in range(KD):
                        act.wait_ge(s.turned, g * KD + k + 1)
                        act.copy(m.outT[:, k, bass.ts(g, BANK)], m.bank[g * KD + k]).then_inc(s.evac, 1)

            @block.sync
            def _(sp):
                sp.dma_start(m.f, io.f[bass.ts(b, 1), :, :, :].rearrange("o p g (i d) -> (o p) (g i) d", d=D)).then_inc(s.f_in, 16)
                sp.dma_start(m.x1, io.x1[bass.ts(b, 1), :, :].rearrange("o (i p) d -> p (o i) d", p=P)).then_inc(s.x_in, 16)
                out = io.out[bass.ts(b, 1), :, :].rearrange("o (i p) d -> p (o i) d", p=P)
                for g in range(PARTS):
                    sp.wait_ge(s.sum, g + 1)
                    sp.dma_start(out[:, bass.ts(g, FT), :], m.x1[:, bass.ts(g, FT), :]).then_inc(s.stored, 16)
                sp.wait_ge(s.stored, 16 * PARTS)
        s.clear()


def build_attention(nc, io):
    with ExitStack() as ctx:
        t = {}

        def sb(name, shape, dt=F32, c=ctx):
            t[name] = c.enter_context(nc.sbuf_tensor("at_" + name, shape, dt))[:]
        ps = ctx.enter_context(nc.psum_tensor("at_ps", [P, 8, BANK], F32))
        t["bank"] = [ps[:, i, :] for i in range(8)]
        t["pair"] = [ps[:, 2 * i:2 * i + 2, :] for i in range(4)]
        sb("ident", [P, P])
        sb("wp", [P, KD, D]); sb("bp", [P, D])
        sb("nlam", [P, 1])
        m = named(**t)
        with ExitStack() as c2:
            for n in ("wq", "wk", "wv"):
                sb(n, [P, KD, D], F32, c2)
            sb("bq", [P, KD], F32, c2); sb("bk", [P, KD], F32, c2); sb("bv", [P, D], F32, c2)
            sb("xT", [P, KD, L], F32, c2); sb("full", [P, 2 * KD, L], F32, c2); sb("r1", [P, 2 * KD, L], F32, c2)
            for n in ("p1", "p2", "p3"):
                sb(n, [P, 2 * KD, L], BF16, c2)
            sb("v", [P, H1, TILES, 32], F32, c2)
            sb("lam", [P, 4, P], F32, c2); sb("lsum", [P, 6, 8], F32, c2); sb("lm", [P, 2], F32, c2)
            m = named(**t)
            s = stage_sems(nc, c2, "at_load", "w_in prod sum low ex diff mean")
            with nc.Block() as block:

                @block.sync
                def _(sp):
                    loads = [(m.ident, io.ident), (m.wq, io.WqT.rearrange("(c p) n -> p c n", p=P)), (m.wk, io.WkT.rearrange("(c p) n -> p c n", p=P)),
                             (m.wv, io.WvT.rearrange("(c p) n -> p c n", p=P)), (m.wp, io.WpT.rearrange("(c p) n -> p c n", p=P)),
                             (m.bv, io.bv.partition_broadcast(P)), (m.bp, io.bp.partition_broadcast(P))]
                    for n, v in enumerate((io.lambda_q1, io.lambda_k1, io.lambda_q2, io.lambda_k2)):
                        loads.append((m.lam[:, n, :], v.rearrange("a b c -> (a b c)").partition_broadcast(P)))
                    with nc.allow_non_contiguous_dma(reason="columns of 128 numbers"):
                        for t, v in ((m.bq, io.bq), (m.bk, io.bk)):
                            sp.dma_start(t, v.rearrange("(c p) -> p c", p=P)).then_inc(s.w_in, 16)
                        for t, v in loads:
                            sp.dma_start(t, v).then_inc(s.w_in, 16)
                    sp.wait_ge(s.w_in, 16 * 13)

                @block.vector
                def _(dve):
                    dve.memset(m.v, 0.0).then_inc(s.prod, 1)
                    dve.wait_ge(s.prod, 1)
                    dve.memset(m.v[:, :, :, HD:HD + 1], 1.0).then_inc(s.prod, 1)
                    dve.wait_ge(s.w_in, 16 * 13)
                    for n in range(2):
                        dve.tensor_tensor(m.lam[:, 2 * n, :], m.lam[:, 2 * n, :], m.lam[:, 2 * n + 1, :], ALU.mult).then_inc(s.prod, 1)
                    dve.wait_ge(s.prod, 4)
                    for n in range(2):
                        dve.tensor_reduce(m.lsum[:, n, :], m.lam[:, 2 * n, :].rearrange("p (h d) -> p h d", d=HD), AX_X, ALU.add).then_inc(s.sum, 1)
                    dve.wait_ge(s.sum, 2)
                    dve.tensor_scalar(m.lsum[:, 2:4, :], m.lsum[:, 0:2, :], 5.0, None, ALU.min).then_inc(s.low, 1)
                    dve.wait_ge(s.ex, 1)
                    dve.tensor_tensor(m.lsum[:, 0, :], m.lsum[:, 4, :], m.lsum[:, 5, :], ALU.subtract).then_inc(s.diff, 1)
                    dve.wait_ge(s.diff, 1)
                    dve.tensor_scalar(m.lsum[:, 1, :], m.lsum[:, 0, :], LAMBDA_INIT, None, ALU.add).then_inc(s.diff, 1)
                    dve.wait_ge(s.diff, 2)
                    dve.tensor_reduce(m.lm[:, 0:1], m.lsum[:, 1, :], AX_X, ALU.add).then_inc(s.mean, 1)
                    dve.wait_ge(s.mean, 1)
                    dve.tensor_scalar(m.nlam, m.lm[:, 0:1], -1.0 / 8, None, ALU.mult).then_inc(s.mean, 1)

                @block.scalar
                def _(act):
                    act.wait_ge(s.low, 1)
                    act.activation(m.lsum[:, 4:6, :], m.lsum[:, 2:4, :], ACT.Exp).then_inc(s.ex, 1)
            s.clear()
            with nc.Fori(0, B) as b:
                project_batch(nc, b, io, m)
        sb("A", [P, HEADS + 1, TILES, HD])
        m = named(**t)
        with ExitStack() as c2:
            sb("E", [P, KT, QB], F32, c2)
            sb("qs", [P, 4, L], BF16, c2)
            sb("ks", [P, 4, L], BF16, c2)
            sb("vst", [P, 2, KT, 32], F32, c2)
            sb("osb", [P, QB], F32, c2)
            sb("selsum", [P, 17], F32, c2)
            sb("mpart", [P, 32], F32, c2); sb("mx", [P, 8], F32, c2); sb("mneg", [8, P], F32, c2)
            sb("mrow", [8, 2, P], BF16, c2); sb("rec", [P, 8, 1], F32, c2)
            sb("y", [P, 2, FT, D], F32, c2); sb("fsum", [P, FT, D], F32, c2); sb("gidx", [P, 2, TILES], U32, c2); sb("gate", [P, 2, TILES], F32, c2)
            sb("gate_in", [P, 2, TILES], F32, c2); sb("units", [P, 2, TILES], F32, c2)
            for n in ("looked_up", "gate_ready", "moved", "gated", "summed"):
                t[n] = c2.enter_context(nc.semaphore(n))
            m = named(**t)
            s = stage_sems(nc, c2, "at_sel", "sel_in")
            with nc.Block() as block:

                @block.sync
                def _(sp):
                    sp.dma_start(m.selsum, io.selsum).then_inc(s.sel_in, 16)
                    sp.wait_ge(s.sel_in, 16)
            s.clear()
            attend(nc, io, m)
        with ExitStack() as c2:
            sb("outT", [P, KD, L], F32, c2)
            sb("mix", [P, TILES, D], F32, c2)
            for n in ("s", "f", "sig", "x1"):
                sb(n, [P, TILES, D], F32, c2)
            m = named(**t)
            with nc.Fori(0, B) as b:
                output_batch(nc, b, io, m)



def build(nc, io):
    build_first_layer(nc, io)
    build_second_ffn(nc, io)
    build_attention(nc, io)


def kernel(**inputs):
    import numpy as np
    import concourse.bacc as bacc
    from concourse.bass_utils import run_bass_kernel_spmd as run

    nc = bacc.Bacc("TRN2", target_bir_lowering=False, num_devices=1)
    arrays, drams = {}, {}

    def put(name, x):
        x = np.ascontiguousarray(x)
        arrays[f"in_{name}"] = x
        drams[name] = nc.dram_tensor(f"in_{name}", x.shape, mybir.dt.from_np(x.dtype), kind="ExternalInput").ap()

    def scratch(name, shape, dt):
        drams[name] = nc.dram_tensor(name, shape, dt, kind="Internal").ap()

    for name, x in inputs.items():
        layer, part, short = name.split("_", 2)
        if layer == "L0":
            put(short, x)
        elif part == "attn" and short[0] == "W":
            put(short + "T", np.asarray(x).T)
        elif part == "attn":
            put(short, x)
        elif short == "Wg":
            put("WgT", np.asarray(x).T)
        else:
            put("e" + short, x)
    put("ident", np.eye(P, dtype=np.float32))
    sel = np.zeros((3, 2 * NS, 2 * NS, P), np.float32)
    for n in range(2 * NS):
        sel[:, n, n, :] = 1
    put("sel", sel.reshape(96, -1).astype(np.dtype("bfloat16")))
    selsum = np.zeros((4, 32, 17), np.float32)
    for c in range(17):
        selsum[:, c, c] = 1
    put("selsum", selsum.reshape(P, 17))
    put("before", np.triu(np.ones((P, P), np.float32), 1))
    put("eid", np.tile(np.arange(E1, dtype=np.float32), (P, 1)))

    scratch("x1", (B, L, D), F32)
    scratch("xn", (B, L, D), F32)
    scratch("xnT", (B, KD, P, L), F32)
    scratch("qp", (B, H1, 3, HD, L), BF16)
    scratch("kp", (B, H1, 3, HD, L), BF16)
    scratch("vp", (B, H1, P, TILES * 32), F32)
    scratch("f", (B, P, TILES // FT, FT * D), F32)
    scratch("xd", (SLOTS, D), F32)
    scratch("yd", (SLOTS, D), F32)
    scratch("places", (B, P, 2, TILES), U32)
    scratch("gates", (B, P, 2, TILES), F32)
    drams["out"] = nc.dram_tensor("out_0", (B, L, D), F32, kind="ExternalOutput").ap()
    build(nc, named(**drams))
    r = run(nc, [arrays], core_ids=[0])
    return r.results[0]["out_0"]
```
